# Optimizing a Trainium2 kernel written in Bass

```python
import numpy as np
import jax
import jax.numpy as jnp

def _softmax(x, axis=-1):
    return jax.nn.softmax(x, axis=axis)

def _gelu(x):
    return jax.nn.gelu(x, approximate=True)

def _silu(x):
    return jax.nn.silu(x)

def _sigmoid(x):
    return jax.nn.sigmoid(x)

def _layernorm(x, axis=-1, eps=1e-05):
    m = jnp.mean(x, axis=axis, keepdims=True)
    v = jnp.var(x, axis=axis, keepdims=True)
    return (x - m) / jnp.sqrt(v + eps)

def _scatter_add(tgt, idx, src, axis=0):
    return tgt.at[idx].add(src)

def _segment_sum(src, seg, n):
    return jax.ops.segment_sum(src, seg, n)
kernel_name = 'mk_flamingo_gated_d1_seqx_r4_d6c0cb'

def setup_inputs(seed: int=0):
    np.random.seed(seed)
    _w = jnp.asarray

    def _rec_inputs():
        import jax
        import jax.numpy as jnp
        _rk = jax.random.key(seed)
        x = 7.22e-05 + 1 * jax.random.normal(jax.random.fold_in(_rk, 1), (8, 256, 256), jnp.float32)
        _lenS = 256 - jax.random.randint(jax.random.fold_in(_rk, 7), (8,), 0, max(1, 256 // 4) + 1, jnp.int32)
        _lenS2 = 120 - jax.random.randint(jax.random.fold_in(_rk, 8), (8,), 0, max(1, 120 // 4) + 1, jnp.int32)
        _ctx_1024P = jax.random.normal(jax.random.fold_in(_rk, 11), (8, 16, 256), jnp.float32)
        _ctx_1024c = jax.random.dirichlet(jax.random.fold_in(_rk, 511), 0.3 * jnp.ones((16,), jnp.float32), (8, 120))
        _ctx_1024t = jnp.einsum('bsk,bkd->bsd', _ctx_1024c, _ctx_1024P)
        _ctx_1024t = _ctx_1024t * jax.lax.rsqrt(jnp.mean(jnp.square(_ctx_1024t)) + 1e-12) * 0.953939
        ctx_1024 = 4.13588e-05 + 0.999923 * (_ctx_1024t + 0.3 * jax.random.normal(jax.random.fold_in(_rk, 611), (8, 120, 256), jnp.float32))
        _validS = jnp.arange(256)[None, :] < _lenS[:, None]
        _validS2 = jnp.arange(120)[None, :] < _lenS2[:, None]
        _causal = jnp.tril(jnp.ones((256, 256), dtype=bool))
        mask_Bx1xS2_bk0 = jnp.logical_not(jnp.broadcast_to(_validS2[:, None, :], (8, 1, 120)))
        _g = jax.random.normal(jax.random.fold_in(_rk, 9001), (2, 1), jnp.float32)
        _g = jnp.sign(_g) * jnp.maximum(jnp.abs(_g), 1.0) + (_g == 0) * 1.0
        g_xattn = _g[0]
        g_ffn = _g[1]
        return (x, ctx_1024, mask_Bx1xS2_bk0, g_xattn, g_ffn)
    x, ctx_1024, mask_Bx1xS2_bk0, g_xattn, g_ffn = _rec_inputs()

    def _L0_xattn_setup():
        import jax, jax.numpy as jnp
        import numpy as np
        B, S, E, H = (4, 512, 256, 16)
        DH = E // H

        def _make_heads(v, n_heads):
            b, n, e = v.shape
            return jnp.moveaxis(v.reshape(b, n, n_heads, e // n_heads), -2, 0)
        key = jax.random.key(seed)
        k1, k2, k3, k4, k5 = jax.random.split(key, 5)
        return {'query': jax.random.normal(k1, (B, S, E), dtype=jnp.float32), 'key': jax.random.normal(k2, (B, S, E), dtype=jnp.float32), 'value': jax.random.normal(k3, (B, S, E), dtype=jnp.float32), 'mask': jax.random.randint(k4, (B, 1, S), 0, 2).astype(bool), 'W_out': jax.random.normal(k5, (E, E), dtype=jnp.float32) / np.sqrt(E), 'scale': jnp.asarray(1.0, dtype=jnp.float32), 'log_C': jnp.asarray(np.log(10.0), dtype=jnp.float32)}
    _L0_xattn_all = _L0_xattn_setup()
    _L0_xattn_in = {k: v for k, v in _L0_xattn_all.items() if k in ('W_out', 'scale', 'log_C')}
    del _L0_xattn_all

    def _L0_ffn_setup():
        import jax, jax.numpy as jnp
        import numpy as np
        B, P, D, D_MLP, E, K = (2, 512, 256, 1024, 8, 2)
        key = jax.random.key(seed)
        k_x, k_g, k_in, k_out = jax.random.split(key, 4)
        s_in = 1.0 / np.sqrt(D).astype(np.float32)
        s_out = 1.0 / np.sqrt(D_MLP).astype(np.float32)
        return {'x': jax.random.normal(k_x, (B, P, D), dtype=jnp.float32), 'W_gate': jax.random.normal(k_g, (D, E), dtype=jnp.float32) * s_in, 'W_in': jax.random.normal(k_in, (E, D, D_MLP), dtype=jnp.float32) * s_in, 'b_in': jnp.zeros((E, D_MLP), dtype=jnp.float32), 'W_out': jax.random.normal(k_out, (E, D_MLP, D), dtype=jnp.float32) * s_out, 'b_out': jnp.zeros((E, D), dtype=jnp.float32)}
    _L0_ffn_all = _L0_ffn_setup()
    _L0_ffn_in = {k: v for k, v in _L0_ffn_all.items() if k in ('W_gate', 'W_in', 'b_in', 'W_out', 'b_out')}
    del _L0_ffn_all
    return {'x': x, 'ctx_1024': ctx_1024, 'mask_Bx1xS2_bk0': mask_Bx1xS2_bk0, 'g_xattn': g_xattn, 'g_ffn': g_ffn, 'L0_xattn_W_out': _L0_xattn_in['W_out'], 'L0_xattn_scale': _L0_xattn_in['scale'], 'L0_xattn_log_C': _L0_xattn_in['log_C'], 'L0_ffn_W_gate': _L0_ffn_in['W_gate'], 'L0_ffn_W_in': _L0_ffn_in['W_in'], 'L0_ffn_b_in': _L0_ffn_in['b_in'], 'L0_ffn_W_out': _L0_ffn_in['W_out'], 'L0_ffn_b_out': _L0_ffn_in['b_out']}

def reference(x, ctx_1024, mask_Bx1xS2_bk0, g_xattn, g_ffn, L0_xattn_W_out, L0_xattn_scale, L0_xattn_log_C, L0_ffn_W_gate, L0_ffn_W_in, L0_ffn_b_in, L0_ffn_W_out, L0_ffn_b_out):
    import jax
    import jax.numpy as jnp

    def _L0_xattn_ref(query, key, value, mask, W_out, scale, log_C):
        import jax, jax.numpy as jnp
        import numpy as np
        B, S, E, H = (4, 512, 256, 16)
        DH = E // H

        def _make_heads(v, n_heads):
            b, n, e = v.shape
            return jnp.moveaxis(v.reshape(b, n, n_heads, e // n_heads), -2, 0)
        q = _make_heads(query, H)
        k = _make_heads(key, H)
        v = _make_heads(value, H)
        d_k = q.shape[-1]
        u = jnp.einsum('hbqd,hbkd->hbqk', q, k) * scale / np.sqrt(d_k)
        logits = jnp.tanh(u) * jnp.exp(log_C)
        logits = jnp.where(mask, -jnp.inf, logits)
        attn = jax.nn.softmax(logits, axis=-1)
        out_heads = jnp.einsum('hbqk,hbkd->hbqd', attn, v)
        out = jnp.moveaxis(out_heads, 0, -2).reshape(query.shape)
        return out @ W_out.T

    def _L0_ffn_ref(x, W_gate, W_in, b_in, W_out, b_out):
        import jax, jax.numpy as jnp
        import numpy as np
        B, P, D, D_MLP, E, K = (2, 512, 256, 1024, 8, 2)
        gate_logits = jnp.einsum('bpd,de->bpe', x, W_gate)
        top_w, top_idx = jax.lax.top_k(gate_logits, K)
        top_w = jax.nn.softmax(top_w, axis=-1)
        combine = jnp.einsum('bpke,bpk->bpe', jax.nn.one_hot(top_idx, E, dtype=x.dtype), top_w)
        out = jnp.zeros_like(x)
        for e in range(E):
            h = jax.nn.gelu(jnp.einsum('bpd,dm->bpm', x, W_in[e]) + b_in[e], approximate=False)
            y = jnp.einsum('bpm,md->bpd', h, W_out[e]) + b_out[e]
            out = out + combine[..., e, None] * y
        return out
    x = x + jnp.tanh(g_xattn[0]) * _L0_xattn_ref(_layernorm(x, axis=-1), ctx_1024, ctx_1024, mask_Bx1xS2_bk0, L0_xattn_W_out, L0_xattn_scale, L0_xattn_log_C)
    x = x + jnp.tanh(g_ffn[0]) * _L0_ffn_ref(_layernorm(x, axis=-1), L0_ffn_W_gate, L0_ffn_W_in, L0_ffn_b_in, L0_ffn_W_out, L0_ffn_b_out)
    return x

_drawn_inputs = setup_inputs


def setup_inputs(seed=0):
    import zlib

    import numpy as np

    out = dict(_drawn_inputs(seed))
    spreads = {'L0_ffn_b_in': (0.0, 0.1), 'L0_ffn_b_out': (0.0, 0.1)}
    factors = {}
    for name, (base, spread) in spreads.items():
        noise = np.random.default_rng([zlib.crc32(name.encode()), seed]).standard_normal(out[name].shape)
        drawn = base * np.exp(spread * noise) if base else spread * noise
        out[name] = jnp.asarray(drawn.astype(out[name].dtype))
    for name, factor in factors.items():
        out[name] = (out[name] * factor).astype(out[name].dtype)
    return out
```

```python
from contextlib import ExitStack

import concourse.bass as bass
from concourse import mybir


def flamingo_layer(nc, x, ctx_rows, ctx_cols, mask_cols, g_xattn, g_ffn, wo_t, scale, log_c,
                   w_gate, w_in, b_in, w_out, b_out, out):
    f32 = mybir.dt.float32
    i32 = mybir.dt.int32
    u32 = mybir.dt.uint32
    u8 = mybir.dt.uint8
    ALU = mybir.AluOpType
    ACT = mybir.ActivationFunctionType
    AX = mybir.AxisListType

    P = 128
    B, S, D = x.shape
    NK = ctx_rows.shape[1]
    H = 16
    DH = D // H
    DC = D // P
    ST = S // P
    NT = B * ST
    TOK = B * S
    E = w_gate.shape[1]
    F = w_in.shape[2]
    FC = F // P
    TOPK = 2
    EPS = 1e-5
    MASKED = -1e30
    EXP_ROOM = 80.0

    ROWS = 32
    RG = P // ROWS
    HR = ROWS // DH
    GH = 4
    NG = H // GH
    VW = DH + 1

    SLOT = 256
    SS = SLOT // P
    MAXT = TOPK * TOK // SLOT + E
    PAY = D + 4
    NB = TOK // SLOT
    NPAIR = E // 2
    CH = 4
    NC = NT // CH
    HP = FC // 2

    slots_dram = nc.dram_tensor("slot_rows", ((MAXT + 1) * SLOT, PAY), f32, kind="Internal").ap()
    y_dram = nc.dram_tensor("expert_rows", (TOPK * TOK + SLOT, D), f32, kind="Internal").ap()

    with ExitStack() as stack:
        def sb(name, shape, dt=f32):
            return stack.enter_context(nc.sbuf_tensor(name, shape, dt))

        def sem(name):
            return stack.enter_context(nc.semaphore(name))

        x_all = sb("x_all", [P, NT, D])
        pay = sb("pay", [P, NT, PAY])
        ident = sb("ident", [P, P])
        scal = sb("scal", [P, 4])
        scal2 = sb("scal2", [P, 4])
        ctx_t = sb("ctx_t", [P, DC, HR, B, NK])
        v_raw = sb("v_raw", [NK, B, D])
        v_aug = sb("v_aug", [NK, B, H, VW])
        mask_u8 = sb("mask_u8", [NK, B], u8)
        key_bias = sb("key_bias", [NK, B])
        bias_now = [sb(f"bias_now{i}", [NK, 1]) for i in range(2)]
        shift = sb("shift", [P, 1])
        wo_sb = sb("wo_sb", [P, DC, D])
        wg_sb = sb("wg_sb", [P, DC, E])
        probs_mem = sb("probs_mem", [P, 2 * H * S])
        probs = probs_mem[0:NK, :].rearrange("k (i h q) -> k i h q", i=2, h=H)
        keys = [sb(f"keys{i}", [P, DC, HR, NK]) for i in range(2)]
        xn = [sb(f"xn{i}", [P, ST, D]) for i in range(2)]
        q_t = [sb(f"q_t{i}", [P, DC, S]) for i in range(2)]
        bn1 = sb("bn1", [P, ST, 6])
        mv1 = sb("mv1", [P, ST, 2])
        ve1 = sb("ve1", [P, ST])
        rstd1 = sb("rstd1", [P, ST])
        bn2 = sb("bn2", [P, ST, 6])
        mv2 = sb("mv2", [P, ST, 2])
        ve2 = sb("ve2", [P, ST])
        rstd2 = sb("rstd2", [P, ST])
        minus_half = sb("minus_half", [P, ST])
        rsum = sb("rsum", [P, ST, H])
        att = sb("att", [P, ST, D])
        att_t = sb("att_t", [P, DC, S])
        xn2 = sb("xn2", [P, ST, D])
        xn2_t = sb("xn2_t", [P, DC, S])
        lg = sb("lg", [P, ST, E])
        top_v = sb("top_v", [P, ST, 8])
        top_i = sb("top_i", [P, ST, 8], u32)
        top_all = sb("top_all", [P, NT, TOPK])
        idx_all = sb("idx_all", [P, NT, TOPK])
        tri = sb("tri", [P, P])
        ones = sb("ones", [P, P])
        tok_id = sb("tok_id", [P, NT], i32)
        e_iota = sb("e_iota", [P, E, NT])
        t_iota = sb("t_iota", [P, E, NB])
        not_first = sb("not_first", [P, E, NT])
        gap = sb("gap", [P, NT])
        egap = sb("egap", [P, NT])
        den = sb("den", [P, NT])
        oh = [sb(f"oh{k}", [P, E, NT]) for k in range(TOPK)]
        member = sb("member", [P, E, NT])
        scan = sb("scan", [P, E, NT])
        more = sb("more", [P, E, NB])
        n_tiles = sb("n_tiles", [P, E])
        n_scan = sb("n_scan", [P, E])
        start = sb("start", [P, E])
        slot_all = sb("slot_all", [P, E, NT])
        slot_f = sb("slot_f", [P, TOPK, NT])
        slot_i = sb("slot_i", [P, TOPK, NT], i32)
        plan = sb("plan", [1, 2 * E + 1], i32)
        w_in_sb = [sb(f"w_in_sb{i}", [P, DC, F]) for i in range(2)]
        w_out_sb = [sb(f"w_out_sb{i}", [P, FC, D]) for i in range(2)]
        b_in_sb = sb("b_in_sb", [P, E, FC])
        b_in_now = sb("b_in_now", [P, FC])
        b_out_sb = sb("b_out_sb", [P, E, D])
        pad = sb("pad", [P, SS, PAY])
        xs = sb("xs", [P, SS, PAY])
        xs_t = sb("xs_t", [P, DC, SLOT])
        hid = sb("hid", [P, FC, SLOT])
        second = sb("second", [P, SS])
        wdiff = sb("wdiff", [P, SS])
        wgt = sb("wgt", [P, SS])
        dest_f = sb("dest_f", [P, SS])
        dest_i = sb("dest_i", [P, SS], i32)
        y_sb = sb("y_sb", [P, SS, D])

        bank = stack.enter_context(nc.psum_tensor("bank", [P, 8, 512], f32))
        SC = bank[:, 0:4, :]
        TQ = bank[:, 4, :]
        AT = bank[:, 5, :]
        AV = [bank[:, 6 + s, :] for s in range(ST)]
        HB = [bank[:, i, :] for i in range(HP)]
        XT = bank[:, 4, :]
        RK = bank[:, 5, :]
        YB = [bank[:, 6 + s, :] for s in range(SS)]

        x_in = [sem(f"x_in{c}") for c in range(NC)]
        scal_in, mask_in, keys_in, v_in, wo_in, wg_in, bias_in = (
            sem(n) for n in ("scal_in", "mask_in", "keys_in", "v_in", "wo_in", "wg_in", "bias_in"))
        ident_done, consts_done, keys_zero, v_done, pool_step = (
            sem(n) for n in ("ident_done", "consts_done", "keys_zero", "v_done", "pool_step"))
        scal_done, c_done, shift_done, bias_done = (
            sem(n) for n in ("scal_done", "c_done", "shift_done", "bias_done"))
        bn1_done, mv1_done, rstd1_done, xn_done, tq_done, qt_done, keys_done = (
            sem(n) for n in ("bn1_done", "mv1_done", "rstd1_done", "xn_done", "tq_done", "qt_done",
                             "keys_done"))
        ve1_done, ve2_done = sem("ve1_done"), sem("ve2_done")
        sc_done, tanh_done, exp_done, av_done, rsum_done, att_done = (
            sem(n) for n in ("sc_done", "tanh_done", "exp_done", "av_done", "rsum_done", "att_done"))
        ta_done, att_t_done, proj_done, x2_done, bn2_done, mv2_done, rstd2_done, xn2_done = (
            sem(n) for n in ("ta_done", "att_t_done", "proj_done", "x2_done", "bn2_done", "mv2_done",
                             "rstd2_done", "xn2_done"))
        pay_done, t2_done, xn2_t_done, gate_done, lg_done, topv_done, topi_done = (
            sem(n) for n in ("pay_done", "t2_done", "xn2_t_done", "gate_done", "lg_done", "topv_done",
                             "topi_done"))
        top_done, route_step, gap_done, egap_done, rank_done, tail_done, slots_done, plan_done = (
            sem(n) for n in ("top_done", "route_step", "gap_done", "egap_done", "rank_done",
                             "tail_done", "slots_done", "plan_done"))
        member_done, b_in_done = sem("member_done"), sem("b_in_done")
        pad_done, pad_out, sent = sem("pad_done"), sem("pad_out"), sem("sent")
        w_in_in = [sem(f"w_in_in{i}") for i in range(2)]
        w_out_in = [sem(f"w_out_in{i}") for i in range(2)]
        xs_in, meta_done, tx_done, xs_t_done, h_done, gelu_done, y_done, y_sb_done = (
            sem(n) for n in ("xs_in", "meta_done", "tx_done", "xs_t_done", "h_done", "gelu_done",
                             "y_done", "y_sb_done"))
        second_done, yb_done, y_sent, y_free = (
            sem(n) for n in ("second_done", "yb_done", "y_sent", "y_free"))
        sum_in = [sem(f"sum_in{c}") for c in range(NC)]
        half_done, sum_done, out_sent = sem("half_done"), sem("sum_done"), sem("out_sent")

        x_view = x.rearrange("b (s p) d -> p (b s) d", p=P)
        out_view = out.rearrange("b (s p) d -> p (b s) d", p=P)
        slots_view = slots_dram.rearrange("(t s p) w -> t p s w", s=SS, p=P)
        y_view = y_dram[0:TOPK * TOK, :].rearrange("(k t p) d -> p k t d", k=TOPK, p=P)
        w_in_view = w_in.rearrange("e (c p) f -> e p c f", p=P)
        w_out_view = w_out.rearrange("e (c p) d -> e p c d", p=P)
        sum_buf = probs_mem[:, :].rearrange("p (c k t d) -> p c k t d", c=NC, k=TOPK, t=CH)

        block = stack.enter_context(nc.Block())

        def value(eng, v):
            return v if type(v) is int else eng.to_reg(v)

        @block.sync
        def _(sp):
            for c in range(1):
                sp.dma_start(x_all[:, c * CH:(c + 1) * CH, :], x_view[:, c * CH:(c + 1) * CH, :]
                             ).then_inc(x_in[c], 16)
            for n, s in enumerate((scale, log_c, g_xattn, g_ffn)):
                sp.dma_start(scal[:, n:n + 1], s.partition_broadcast(P)).then_inc(scal_in, 16)
            sp.dma_start(mask_u8[:, :], mask_cols).then_inc(mask_in, 16)
            sp.wait_ge(keys_zero, 1)
            for h in range(H):
                c, rg, hr = h // (RG * HR), (h // HR) % RG, h % HR
                p0 = rg * ROWS + hr * DH
                sp.dma_start(ctx_t[p0:p0 + DH, c, hr, :, :], ctx_cols[h * DH:(h + 1) * DH, :, :]
                             ).then_inc(keys_in, 16)
            sp.dma_start(v_raw[:, :, :], ctx_rows.rearrange("b k d -> k b d")).then_inc(v_in, 16)
            for c in range(1, NC):
                sp.dma_start(x_all[:, c * CH:(c + 1) * CH, :], x_view[:, c * CH:(c + 1) * CH, :]
                             ).then_inc(x_in[c], 16)
            sp.dma_start(wo_sb[:, :, :], wo_t.rearrange("(c p) f -> p c f", p=P)).then_inc(wo_in, 16)
            sp.dma_start(wg_sb[:, :, :], w_gate.rearrange("(c p) e -> p c e", p=P)).then_inc(wg_in, 16)
            sp.dma_start(b_in_sb[:, :, :], b_in).then_inc(bias_in, 16)
            sp.dma_start(b_out_sb[:, :, :], b_out.partition_broadcast(P)).then_inc(bias_in, 16)
            sp.wait_ge(pad_done, 4)
            for t in range(MAXT + 1):
                sp.dma_start(slots_view[t], pad[:, :, :]).then_inc(pad_out, 16)
            sp.wait_ge(sent, 16 * TOPK * NT)
            sp.wait_ge(plan_done, 1)
            total = sp.value_load(plan[0:1, 2 * E:2 * E + 1], min_val=E, max_val=MAXT)
            sp.dma_start(xs[:, :, :], slots_view[0]).then_inc(xs_in, 16)
            with sp.Fori(1, total + 1) as t:
                sp.wait_ge(meta_done, t)
                sp.wait_ge(tx_done, t)
                sp.dma_start(xs[:, :, :], slots_view[t]).then_inc(xs_in, 16)
            sp.wait_ge(y_sent, total * (16 * SS))
            for c in range(NC):
                for k in range(TOPK):
                    sp.dma_start(sum_buf[:, c, k, :, :], y_view[:, k, c * CH:(c + 1) * CH, :]
                                 ).then_inc(sum_in[c], 16)

        @block.gpsimd
        def _(pool):
            pool.memset(ident[:, :], 0.0).then_inc(pool_step, 1)
            pool.wait_ge(pool_step, 1)
            pool.affine_select(out=ident[:, :], in_=ident[:, :], compare_op=ALU.not_equal, fill=1.0, base=0,
                               pattern=[[-1, P]], channel_multiplier=1).then_inc(ident_done, 1)
            pool.memset(minus_half[:, :], -0.5).then_inc(pool_step, 1)
            pool.memset(v_aug[:, :, :, :], 1.0).then_inc(pool_step, 1)

            def key_rows(b, i):
                if type(b) is not int or b >= 2:
                    pool.wait_ge(sc_done, (b - 1) * NG)
                    pool.wait_ge(exp_done, (b - 1) * 2)
                pool.tensor_copy(bias_now[i][:, :], key_bias[:, bass.ds(b, 1)])
                pool.tensor_copy(keys[i][:, :, :, :], ctx_t[:, :, :, b, :]).then_inc(keys_done, 1)

            def rstd(b, mv, ve, done_in, ve_done, r, done_out):
                after = value(pool, b + 1)
                pool.wait_ge(keys_in, 16 * H)
                pool.wait_ge(done_in, after)
                pool.tensor_scalar(ve[:, :], mv[:, :, 1], EPS, None, ALU.add).then_inc(ve_done, 1)
                pool.wait_ge(ve_done, b + 1)
                pool.tensor_tensor(r[:, :], ve[:, :], minus_half[:, :], ALU.pow).then_inc(done_out, 1)

            def front(b, i):
                rstd(b, mv1, ve1, mv1_done, ve1_done, rstd1, rstd1_done)
                key_rows(b, i)

            def back(b):
                rstd(b, mv2, ve2, mv2_done, ve2_done, rstd2, rstd2_done)
                pool.wait_ge(xn2_done, b + 1)
                pool.tensor_copy(pay[:, bass.ds(b * ST, ST), 0:D], xn2[:, :, :]).then_inc(pay_done, 1)

            pool.wait_ge(keys_in, 16 * H)
            pool.wait_ge(pool_step, 3)
            pool.wait_ge(bias_done, 1)
            front(0, 0)
            front(1, 1)
            pool.wait_ge(v_in, 16)
            pool.tensor_copy(v_aug[:, :, :, 0:DH], v_raw[:, :, :].rearrange("k b (h d) -> k b h d", h=H)
                             ).then_inc(v_done, 1)
            pool.memset(pad[:, :, 0:D + 2], 0.0).then_inc(pad_done, 1)
            pool.memset(pad[:, :, D + 2:D + 3], -1.0).then_inc(pad_done, 1)
            for s in range(SS):
                pool.iota(pad[:, s, D + 3:D + 4], [[0, 1]], base=TOK + s * P, channel_multiplier=1,
                          allow_small_or_imprecise_dtypes=True).then_inc(pad_done, 1)
            pool.memset(ones[:, :], 1.0)
            pool.memset(not_first[:, :, :], 1.0).then_inc(pool_step, 1)
            pool.wait_ge(pool_step, 4)
            pool.memset(not_first[:, :, 0:1], 0.0)
            pool.affine_select(out=tri[:, :], in_=ones[:, :], compare_op=ALU.is_gt, fill=0.0, base=0,
                               pattern=[[1, P]], channel_multiplier=-1)
            pool.iota(tok_id[:, :], [[P, NT]], base=0, channel_multiplier=1)
            pool.iota(e_iota[:, :, :], [[1, E], [0, NT]], base=0, channel_multiplier=0,
                      allow_small_or_imprecise_dtypes=True)
            pool.iota(t_iota[:, :, :], [[0, E], [SLOT, NB]], base=0, channel_multiplier=0,
                      allow_small_or_imprecise_dtypes=True).then_inc(consts_done, 1)
            with pool.Fori(0, (B - 2) // 2) as i:
                front(2 * i + 2, 0)
                back(2 * i)
                front(2 * i + 3, 1)
                back(2 * i + 1)
            back(B - 2)
            back(B - 1)
            pool.wait_ge(pad_out, 16 * (MAXT + 1))
            pool.wait_ge(tail_done, 1)
            pool.wait_ge(pay_done, B)
            pool.wait_ge(slots_done, 1)
            for j in range(NT):
                for k in range(TOPK):
                    pool.indirect_dma_start(
                        out=slots_dram, out_offset=bass.IndirectOffsetOnAxis(ap=slot_i[:, k, j:j + 1], axis=0),
                        in_=pay[:, j, :], in_offset=None).then_inc(sent, 16)
            pool.wait_ge(plan_done, 1)
            total = pool.value_load(plan[0:1, 2 * E:2 * E + 1], min_val=E, max_val=MAXT)
            pool.nop().then_inc(y_free, 1)
            with pool.Fori(0, total) as t:
                after = value(pool, t + 1)
                pool.wait_ge(plan_done, 1)
                pool.wait_ge(y_sb_done, after)
                for s in range(SS):
                    pool.indirect_dma_start(
                        out=y_dram, out_offset=bass.IndirectOffsetOnAxis(ap=dest_i[:, s:s + 1], axis=0),
                        in_=y_sb[:, s, :], in_offset=None).then_inc(y_sent, 16)
                pool.wait_ge(y_sent, t * (16 * SS) + 16 * SS)
                pool.nop().then_inc(y_free, 1)

        @block.scalar
        def _(act):
            for e in range(2):
                act.dma_start(w_in_sb[e][:, :, :], w_in_view[e]).then_inc(w_in_in[e], 16)
                act.dma_start(w_out_sb[e][:, :, :], w_out_view[e]).then_inc(w_out_in[e], 16)
            act.wait_ge(scal_in, 64)
            act.activation(scal2[:, 2:4], scal[:, 2:4], ACT.Tanh).then_inc(scal_done, 1)
            act.activation(scal2[:, 0:1], scal[:, 0:1], ACT.Copy, scale=float(DH) ** -0.5
                           ).then_inc(scal_done, 1)
            act.activation(scal2[:, 1:2], scal[:, 1:2], ACT.Exp).then_inc(c_done, 1)
            act.wait_ge(scal_done, 2)
            act.wait_ge(c_done, 1)
            act.wait_ge(bias_done, 1)

            def soften(b, i):
                for g in range(NG):
                    if g == 0 and (type(b) is not int or b >= 2):
                        act.wait_ge(av_done, b - 1)
                    act.wait_ge(sc_done, b * NG + (g + 1))
                    r0 = GH // HR * (g % 2)
                    act.activation(probs[:, i, g * GH:(g + 1) * GH, :],
                                   SC[0:NK, r0:r0 + GH // HR, :].rearrange("k r (h q) -> k (r h) q", q=S),
                                   ACT.Tanh, scale=scal2[0:NK, 0:1]).then_inc(tanh_done, 1)
                    if g % 2:
                        act.wait_ge(tanh_done, b * NG + (g + 1))
                        both = probs[:, i, (g - 1) * GH:(g + 1) * GH, :]
                        act.activation(both, both, ACT.Exp, bias=bias_now[i][:, :],
                                       scale=scal2[0:NK, 1:2]).then_inc(exp_done, 1)

            soften(0, 0)
            soften(1, 1)
            with act.Fori(0, (B - 2) // 2) as i:
                soften(2 * i + 2, 0)
                soften(2 * i + 3, 1)
            act.wait_ge(gap_done, 1)
            act.activation(egap[:, :], gap[:, :], ACT.Exp).then_inc(egap_done, 1)

            def next_weights(e, i, after):
                act.wait_ge(y_done, after)
                act.dma_start(w_in_sb[i][:, :, :], w_in_view[e + 2]).then_inc(w_in_in[i], 16)
                act.dma_start(w_out_sb[i][:, :, :], w_out_view[e + 2]).then_inc(w_out_in[i], 16)

            def expert(e):
                first = act.value_load(plan[0:1, bass.ds(e, 1)], min_val=0, max_val=MAXT)
                count = act.value_load(plan[0:1, bass.ds(e + E, 1)], min_val=1, max_val=NB)
                act.activation(b_in_now[:, :], b_in_sb[:, bass.ds(e, 1), :].squeeze(1), ACT.Copy).then_inc(b_in_done, 1)
                act.wait_ge(b_in_done, e + 1)
                with act.Fori(0, count) as t:
                    for m in range(FC):
                        if m % 2 == 0:
                            act.wait_ge(h_done, (first + t) * HP + (m // 2 + 1))
                        ins = act.activation(hid[:, m, :], HB[m // 2][:, (m % 2) * SLOT:(m % 2 + 1) * SLOT],
                                             ACT.Gelu, bias=b_in_now[:, m:m + 1])
                        if m % 2:
                            ins.then_inc(gelu_done, 1)
                after = value(act, (first + count) * HP)
                act.wait_ge(bias_in, 32)
                act.wait_ge(gelu_done, after)
                return first + count

            act.wait_ge(bias_in, 32)
            act.wait_ge(plan_done, 1)
            with act.Fori(0, NPAIR - 1) as i:
                next_weights(2 * i, 0, expert(2 * i))
                next_weights(2 * i + 1, 1, expert(2 * i + 1))
            expert(E - 2)
            expert(E - 1)
            for c in range(NC):
                act.wait_ge(sum_done, c + 1)
                act.dma_start(out_view[:, c * CH:(c + 1) * CH, :], sum_buf[:, c, 0, :, :]
                              ).then_inc(out_sent, 16)
            act.wait_ge(out_sent, 16 * NC)

        @block.vector
        def _(dve):
            dve.memset(ctx_t[:, :, :, :, :], 0.0).then_inc(keys_zero, 1)
            dve.wait_ge(c_done, 1)
            dve.tensor_scalar(shift[:, :], scal2[:, 1:2], -1.0, EXP_ROOM, ALU.mult, ALU.add
                              ).then_inc(shift_done, 1)
            dve.wait_ge(shift_done, 1)
            dve.tensor_scalar(shift[:, :], shift[:, :], 0.0, None, ALU.min).then_inc(shift_done, 1)
            dve.wait_ge(shift_done, 2)
            dve.wait_ge(mask_in, 16)
            dve.tensor_scalar(key_bias[:, :], mask_u8[:, :], MASKED, shift[0:NK, :], ALU.mult, ALU.add
                              ).then_inc(bias_done, 1)

            def stats(b, xs_of, bn, mv, bnd, mvd):
                after = value(dve, b + 1)
                dve.wait_ge(x_in[NC - 1], 16)
                if bnd is bn2_done:
                    dve.wait_ge(x2_done, after)
                for s in range(ST):
                    ins = dve.bn_stats(bn[:, s, :], xs_of(s))
                ins.then_inc(bnd, 1)
                dve.wait_ge(x_in[NC - 1], 16)
                dve.wait_ge(bnd, after)
                for s in range(ST):
                    ins = dve.bn_aggr(mv[:, s, :], bn[:, s, :])
                ins.then_inc(mvd, 1)

            def stats1(b):
                stats(b, lambda s: x_all[:, bass.ds(b * ST + s, 1), :].squeeze(1), bn1, mv1, bn1_done, mv1_done)

            def norm1(b, i):
                dve.wait_ge(rstd1_done, b + 1)
                for s in range(ST):
                    ins = dve.tensor_scalar(xn[i][:, s, :], x_all[:, bass.ds(b * ST + s, 1), :].squeeze(1),
                                            mv1[:, s, 0:1], rstd1[:, s:s + 1], ALU.subtract, ALU.mult)
                ins.then_inc(xn_done, 1)

            def query(b, i):
                dve.wait_ge(tq_done, b + 1)
                dve.tensor_copy(q_t[i][:, :, :], TQ.rearrange("p (c q) -> p c q", c=DC)).then_inc(qt_done, 1)

            def attend(b):
                dve.wait_ge(av_done, b + 1)
                for s in range(ST):
                    ins = dve.reciprocal(rsum[:, s, :], AV[s][:, 0:H * VW].rearrange("p (h w) -> p h w", w=VW)[:, :, DH])
                ins.then_inc(rsum_done, 1)
                dve.wait_ge(rsum_done, b + 1)
                for s in range(ST):
                    ins = dve.tensor_tensor(
                        att[:, s, :].rearrange("p (h d) -> p h d", h=H),
                        AV[s][:, 0:H * VW].rearrange("p (h w) -> p h w", w=VW)[:, :, 0:DH],
                        rsum[:, s, :].unsqueeze(2).to_broadcast([P, H, DH]), ALU.mult)
                ins.then_inc(att_done, 1)

            def att_turned(b):
                dve.wait_ge(ta_done, b + 1)
                dve.tensor_copy(att_t[:, :, :], AT.rearrange("p (c q) -> p c q", c=DC)).then_inc(att_t_done, 1)

            def residual(b):
                dve.wait_ge(proj_done, b + 1)
                for s in range(ST):
                    row = x_all[:, bass.ds(b * ST + s, 1), :].squeeze(1)
                    ins = dve.scalar_tensor_tensor(row, AT[:, s * D:(s + 1) * D], scal2[:, 2:3], row,
                                                   ALU.mult, ALU.add)
                ins.then_inc(x2_done, 1)
                stats(b, lambda s: x_all[:, bass.ds(b * ST + s, 1), :].squeeze(1), bn2, mv2, bn2_done, mv2_done)

            def norm2(b):
                dve.wait_ge(rstd2_done, b + 1)
                if type(b) is not int or b >= 1:
                    dve.wait_ge(pay_done, b)
                for s in range(ST):
                    ins = dve.tensor_scalar(xn2[:, s, :], x_all[:, bass.ds(b * ST + s, 1), :].squeeze(1),
                                            mv2[:, s, 0:1], rstd2[:, s:s + 1], ALU.subtract, ALU.mult)
                ins.then_inc(xn2_done, 1)

            def xn2_turned(b):
                dve.wait_ge(t2_done, b + 1)
                dve.tensor_copy(xn2_t[:, :, :], TQ.rearrange("p (c q) -> p c q", c=DC)).then_inc(xn2_t_done, 1)

            def choose(b):
                dve.wait_ge(gate_done, b + 1)
                dve.tensor_copy(lg[:, :, :], TQ[:, 0:ST * E].rearrange("p (s e) -> p s e", s=ST)).then_inc(lg_done, 1)
                after = value(dve, b + 1)
                dve.wait_ge(x_in[NC - 1], 16)
                dve.wait_ge(lg_done, after)
                for s in range(ST):
                    ins = dve.max(top_v[:, s, :], lg[:, s, :])
                ins.then_inc(topv_done, 1)
                dve.wait_ge(x_in[NC - 1], 16)
                dve.wait_ge(topv_done, after)
                for s in range(ST):
                    ins = dve.max_index(top_i[:, s, :], top_v[:, s, :], lg[:, s, :])
                ins.then_inc(topi_done, 1)
                dve.tensor_copy(top_all[:, bass.ds(b * ST, ST), :], top_v[:, :, 0:TOPK])
                dve.wait_ge(topi_done, b + 1)
                dve.tensor_copy(idx_all[:, bass.ds(b * ST, ST), :], top_i[:, :, 0:TOPK]).then_inc(top_done, 1)

            for c in range(NC):
                dve.wait_ge(x_in[c], 16)
            stats1(0)
            norm1(0, 0)
            dve.wait_ge(scal_done, 2)
            query(0, 0)
            stats1(1)
            norm1(1, 1)
            query(1, 1)
            stats1(2)
            norm1(2, 0)
            attend(0)
            att_turned(0)
            residual(0)
            norm2(0)

            def step(b, i, last=False):
                query(b, i)
                if not last:
                    stats1(b + 1)
                    norm1(b + 1, 1 - i)
                attend(b - 1)
                xn2_turned(b - 2)
                att_turned(b - 1)
                choose(b - 2)
                residual(b - 1)
                norm2(b - 1)

            with dve.Fori(0, (B - 4) // 2) as i:
                step(2 * i + 2, 0)
                step(2 * i + 3, 1)
            step(B - 2, 0)
            step(B - 1, 1, last=True)
            attend(B - 1)
            xn2_turned(B - 2)
            att_turned(B - 1)
            choose(B - 2)
            residual(B - 1)
            norm2(B - 1)
            xn2_turned(B - 1)
            choose(B - 1)

            count = [0]

            def link(ins):
                count[0] += 1
                ins.then_inc(route_step, 1)
                dve.wait_ge(route_step, count[0])

            dve.wait_ge(consts_done, 1)
            dve.wait_ge(top_done, B)
            dve.tensor_tensor(gap[:, :], top_all[:, :, 1], top_all[:, :, 0], ALU.subtract).then_inc(gap_done, 1)
            for k in range(TOPK):
                last = dve.tensor_tensor(oh[k][:, :, :], idx_all[:, :, k].unsqueeze(1).to_broadcast([P, E, NT]),
                                         e_iota[:, :, :], ALU.is_equal)
            link(last)
            dve.tensor_tensor(member[:, :, :], oh[0][:, :, :], oh[1][:, :, :], ALU.add).then_inc(member_done, 1)
            dve.wait_ge(egap_done, 1)
            link(dve.tensor_scalar(den[:, :], egap[:, :], 1.0, None, ALU.add))
            link(dve.reciprocal(den[:, :], den[:, :]))
            link(dve.tensor_scalar(pay[:, :, D], den[:, :], scal2[:, 3:4], None, ALU.mult))
            dve.tensor_tensor(pay[:, :, D + 1], pay[:, :, D], egap[:, :], ALU.mult)
            dve.tensor_copy(pay[:, :, D + 2], idx_all[:, :, 0])
            dve.tensor_copy(pay[:, :, D + 3], tok_id[:, :]).then_inc(tail_done, 1)
            dve.wait_ge(rank_done, 1)
            ET = E * NT
            flat = "p e t -> p (e t)"
            link(dve.tensor_tensor_scan(scan[:, :, :].rearrange(flat), not_first[:, :, :].rearrange(flat),
                                        RK[:, ET:2 * ET], 0.0, ALU.mult, ALU.add))
            link(dve.tensor_tensor(more[:, :, :], scan[:, :, NT - 1].unsqueeze(2).to_broadcast([P, E, NB]),
                                   t_iota[:, :, :], ALU.is_gt))
            link(dve.tensor_reduce(n_tiles[:, :], more[:, :, :], axis=AX.X, op=ALU.add))
            link(dve.tensor_scalar(n_tiles[:, :], n_tiles[:, :], 1.0, None, ALU.max))
            link(dve.tensor_tensor_scan(n_scan[:, :], ones[:, 0:E], n_tiles[:, :], 0.0, ALU.mult, ALU.add))
            link(dve.tensor_tensor(start[:, :], n_scan[:, :], n_tiles[:, :], ALU.subtract))
            dve.tensor_copy(plan[0:1, 0:E], start[0:1, :])
            dve.tensor_copy(plan[0:1, E:2 * E], n_tiles[0:1, :])
            dve.tensor_copy(plan[0:1, 2 * E:2 * E + 1], n_scan[0:1, E - 1:E]).then_inc(plan_done, 1)
            link(dve.tensor_tensor(scan[:, :, :].rearrange(flat), scan[:, :, :].rearrange(flat), RK[:, ET:2 * ET],
                                   ALU.subtract))
            link(dve.tensor_tensor(scan[:, :, :].rearrange(flat), scan[:, :, :].rearrange(flat), RK[:, 0:ET],
                                   ALU.add))
            link(dve.scalar_tensor_tensor(slot_all[:, :, :], start[:, :].unsqueeze(2).to_broadcast([P, E, NT]),
                                          float(SLOT), scan[:, :, :], ALU.mult, ALU.add))
            for k in range(TOPK):
                last = dve.tensor_tensor(oh[k][:, :, :], oh[k][:, :, :], slot_all[:, :, :], ALU.mult)
            link(last)
            for k in range(TOPK):
                last = dve.tensor_reduce(slot_f[:, k, :], oh[k][:, :, :].rearrange("p e t -> p t e"), axis=AX.X,
                                         op=ALU.add)
            link(last)
            dve.tensor_copy(slot_i[:, :, :], slot_f[:, :, :]).then_inc(slots_done, 1)

            def turned(t):
                dve.wait_ge(tx_done, t + 1)
                dve.tensor_copy(xs_t[:, :, :], XT.rearrange("p (c q) -> p c q", c=DC)).then_inc(xs_t_done, 1)

            def meta(e, t):
                dve.wait_ge(xs_in, (t + 1) * 16)
                dve.wait_ge(y_free, t + 1)
                dve.tensor_scalar(second[:, :], xs[:, :, D + 2], e_col(e), None, ALU.not_equal
                                  ).then_inc(second_done, 1)
                dve.tensor_tensor(wdiff[:, :], xs[:, :, D + 1], xs[:, :, D], ALU.subtract).then_inc(second_done, 1)
                dve.wait_ge(second_done, 5 * t + 2)
                dve.tensor_tensor(wdiff[:, :], wdiff[:, :], second[:, :], ALU.mult).then_inc(second_done, 1)
                dve.wait_ge(second_done, 5 * t + 3)
                dve.tensor_tensor(wgt[:, :], wdiff[:, :], xs[:, :, D], ALU.add).then_inc(second_done, 1)
                dve.scalar_tensor_tensor(dest_f[:, :], second[:, :], float(TOK), xs[:, :, D + 3], ALU.mult, ALU.add
                                         ).then_inc(second_done, 1)
                dve.wait_ge(second_done, 5 * t + 5)
                dve.tensor_copy(dest_i[:, :], dest_f[:, :]).then_inc(meta_done, 1)

            def e_col(e):
                return e_iota[:, bass.ds(e, 1), 0]

            def expert(e):
                first = dve.value_load(plan[0:1, bass.ds(e, 1)], min_val=0, max_val=MAXT)
                count_e = dve.value_load(plan[0:1, bass.ds(e + E, 1)], min_val=1, max_val=NB)
                with dve.Fori(0, count_e) as t0:
                    t = dve.snap(first + t0)
                    meta(e, t)
                    turned(t + 1)
                    dve.wait_ge(y_done, t + 1)
                    for s in range(SS):
                        ins = dve.tensor_tensor(y_sb[:, s, :], YB[s][:, 0:D], b_out_sb[:, bass.ds(e, 1), :].squeeze(1),
                                                ALU.add)
                    ins.then_inc(yb_done, 1)
                    dve.wait_ge(yb_done, t + 1)
                    for s in range(SS):
                        ins = dve.tensor_scalar(y_sb[:, s, :], y_sb[:, s, :], wgt[:, s:s + 1], None, ALU.mult)
                    ins.then_inc(y_sb_done, 1)

            turned(0)
            with dve.Fori(0, NPAIR) as i:
                expert(2 * i)
                expert(2 * i + 1)
            for c in range(NC):
                dve.wait_ge(sum_in[c], 16 * TOPK)
                a, b2 = sum_buf[:, c, 0, :, :], sum_buf[:, c, 1, :, :]
                dve.tensor_tensor(a, a, b2, ALU.add).then_inc(half_done, 1)
                dve.wait_ge(half_done, c + 1)
                dve.tensor_tensor(a, a, x_all[:, c * CH:(c + 1) * CH, :], ALU.add).then_inc(sum_done, 1)

        @block.tensor
        def _(pe):
            def turn(dst, src):
                for s in range(ST):
                    for c in range(DC):
                        ins = pe.transpose(dst[:, c * S + s * P:c * S + (s + 1) * P], src[:, s, c * P:(c + 1) * P],
                                           ident[:, :])
                return ins

            def turn_queries(b, i):
                pe.wait_ge(xn_done, b + 1)
                if type(b) is not int or b >= 3:
                    pe.wait_ge(lg_done, b - 2)
                if type(b) is int and b == 1:
                    pe.wait_ge(qt_done, 1)
                turn(TQ, xn[i]).then_inc(tq_done, 1)

            def scores(b, i, g):
                if g == 0:
                    pe.wait_ge(qt_done, b + 1)
                    pe.wait_ge(keys_done, b + 1)
                if type(b) is not int or b * NG + g >= 2:
                    pe.wait_ge(tanh_done, b * NG + (g - 1))
                c = g // 2
                for hr in range(HR):
                    for r in range(GH // HR):
                        rg = GH // HR * (g % 2) + r
                        rows = slice(rg * ROWS, (rg + 1) * ROWS)
                        ins = pe.matmul(SC[0:NK, rg, hr * S:(hr + 1) * S], keys[i][rows, c, hr, :], q_t[i][rows, c, :],
                                        start=True, stop=True)
                ins.then_inc(sc_done, 1)

            def values(b, i, half):
                pe.wait_ge(exp_done, 2 * b + (half + 1))
                if half == 0:
                    if type(b) is int and b == 0:
                        pe.wait_ge(v_done, 1)
                    else:
                        pe.wait_ge(att_done, b)
                for s in range(ST):
                    for h in range(half * H // 2, (half + 1) * H // 2):
                        ins = pe.matmul(AV[s][:, h * VW:(h + 1) * VW], probs[:, i, h, s * P:(s + 1) * P],
                                        v_aug[:, bass.ds(b, 1), h, :].squeeze(1), start=True, stop=True)
                if half:
                    ins.then_inc(av_done, 1)

            def turn_att(b):
                pe.wait_ge(att_done, b + 1)
                if type(b) is not int or b >= 1:
                    pe.wait_ge(x2_done, b)
                turn(AT, att).then_inc(ta_done, 1)

            def project(b):
                pe.wait_ge(att_t_done, b + 1)
                for s in range(ST):
                    for c in range(DC):
                        ins = pe.matmul(AT[:, s * D:(s + 1) * D], att_t[:, c, s * P:(s + 1) * P], wo_sb[:, c, :],
                                        start=(c == 0), stop=(c == DC - 1))
                ins.then_inc(proj_done, 1)

            def turn_xn2(b):
                pe.wait_ge(xn2_done, b + 1)
                turn(TQ, xn2).then_inc(t2_done, 1)

            def gate(b):
                pe.wait_ge(xn2_t_done, b + 1)
                for s in range(ST):
                    for c in range(DC):
                        ins = pe.matmul(TQ[:, s * E:(s + 1) * E], xn2_t[:, c, s * P:(s + 1) * P], wg_sb[:, c, :],
                                        start=(c == 0), stop=(c == DC - 1))
                ins.then_inc(gate_done, 1)

            pe.wait_ge(ident_done, 1)
            turn_queries(0, 0)
            for g in range(NG):
                scores(0, 0, g)
            pe.wait_ge(wo_in, 16)
            pe.wait_ge(wg_in, 16)
            turn_queries(1, 1)
            values(0, 0, 0)
            scores(1, 1, 0)
            values(0, 0, 1)
            scores(1, 1, 1)
            turn_att(0)
            scores(1, 1, 2)
            project(0)
            scores(1, 1, 3)

            def step(b, i):
                turn_queries(b, i)
                values(b - 1, 1 - i, 0)
                scores(b, i, 0)
                values(b - 1, 1 - i, 1)
                scores(b, i, 1)
                turn_xn2(b - 2)
                turn_att(b - 1)
                scores(b, i, 2)
                gate(b - 2)
                project(b - 1)
                scores(b, i, 3)

            step(2, 0)
            step(3, 1)
            with pe.Fori(0, (B - 4) // 2) as i:
                step(2 * i + 4, 0)
                step(2 * i + 5, 1)
            values(B - 1, 1, 0)
            values(B - 1, 1, 1)
            pe.wait_ge(lg_done, B - 2)
            turn_xn2(B - 2)
            turn_att(B - 1)
            gate(B - 2)
            project(B - 1)
            pe.wait_ge(lg_done, B - 1)
            turn_xn2(B - 1)
            gate(B - 1)

            pe.wait_ge(member_done, 1)
            pe.wait_ge(x2_done, B)
            ET = E * NT
            flat = member[:, :, :].rearrange("p e t -> p (e t)")
            pe.matmul(RK[:, 0:ET], tri[:, :], flat, start=True, stop=True)
            pe.matmul(RK[:, ET:2 * ET], ones[:, :], flat, start=True, stop=True).then_inc(rank_done, 1)

            def turn_slots(t):
                pe.wait_ge(xs_in, (t + 1) * 16)
                for s in range(SS):
                    for c in range(DC):
                        ins = pe.transpose(XT[:, c * SLOT + s * P:c * SLOT + (s + 1) * P], xs[:, s, c * P:(c + 1) * P],
                                           ident[:, :])
                ins.then_inc(tx_done, 1)

            def expert(e, i, pair):
                first = pe.value_load(plan[0:1, bass.ds(e, 1)], min_val=0, max_val=MAXT)
                count = pe.value_load(plan[0:1, bass.ds(e + E, 1)], min_val=1, max_val=NB)
                loads = value(pe, (pair + 1) * 16)
                pe.wait_ge(plan_done, 1)
                pe.wait_ge(w_in_in[i], loads)
                pe.wait_ge(w_out_in[i], loads)
                with pe.Fori(0, count) as t0:
                    t = pe.snap(first + t0)
                    pe.wait_ge(xs_t_done, t + 1)
                    for m in range(FC):
                        for c in range(DC):
                            ins = pe.matmul(HB[m // 2][:, (m % 2) * SLOT:(m % 2 + 1) * SLOT],
                                            w_in_sb[i][:, c, m * P:(m + 1) * P], xs_t[:, c, :],
                                            start=(c == 0), stop=(c == DC - 1))
                        if m % 2:
                            ins.then_inc(h_done, 1)
                    turn_slots(t + 1)
                    pe.wait_ge(meta_done, t + 1)
                    for m in range(FC):
                        if m % 2 == 0:
                            pe.wait_ge(gelu_done, t * HP + (m // 2 + 1))
                        for s in range(SS):
                            ins = pe.matmul(YB[s][:, 0:D], hid[:, m, s * P:(s + 1) * P], w_out_sb[i][:, m, :],
                                            start=(m == 0), stop=(m == FC - 1))
                    ins.then_inc(y_done, 1)

            pe.wait_ge(lg_done, B)
            turn_slots(0)
            pe.wait_ge(plan_done, 1)
            with pe.Fori(0, NPAIR) as i:
                expert(2 * i, 0, i)
                expert(2 * i + 1, 1, i)


_OUT = (8, 256, 256)


def kernel(**inputs):
    import numpy as np
    import concourse.bacc as bacc
    from concourse.bass_utils import run_bass_kernel_spmd

    a = {k: np.asarray(v) for k, v in inputs.items()}
    ctx = a["ctx_1024"]
    laid_out = {
        "x": a["x"],
        "ctx_rows": ctx,
        "ctx_cols": np.ascontiguousarray(ctx.transpose(2, 0, 1)),
        "mask_cols": np.ascontiguousarray(a["mask_Bx1xS2_bk0"][:, 0, :].T),
        "g_xattn": a["g_xattn"].reshape(1),
        "g_ffn": a["g_ffn"].reshape(1),
        "wo_t": np.ascontiguousarray(a["L0_xattn_W_out"].T),
        "scale": a["L0_xattn_scale"].reshape(1),
        "log_c": a["L0_xattn_log_C"].reshape(1),
        "w_gate": a["L0_ffn_W_gate"],
        "w_in": a["L0_ffn_W_in"],
        "b_in": np.ascontiguousarray(a["L0_ffn_b_in"].reshape(8, 8, 128).transpose(2, 0, 1)),
        "w_out": a["L0_ffn_W_out"],
        "b_out": a["L0_ffn_b_out"],
    }
    nc = bacc.Bacc("TRN2", target_bir_lowering=False, num_devices=1)
    aps = {n: nc.dram_tensor(n, v.shape, mybir.dt.from_np(v.dtype), kind="ExternalInput").ap()
           for n, v in laid_out.items()}
    out = nc.dram_tensor("out", _OUT, mybir.dt.float32, kind="ExternalOutput").ap()
    flamingo_layer(nc, out=out, **aps)
    r = run_bass_kernel_spmd(nc, [laid_out], core_ids=[0])
    return r.results[0]["out"]
```

```python
from contextlib import ExitStack

import concourse.bass as bass
from concourse import mybir


def flamingo_layer(nc, x, keys_dram, vals_dram, mask_cols, scalars, wo_t, w_gate, w_in, b_in,
                   w_out, b_out, out):
    f32 = mybir.dt.float32
    i32 = mybir.dt.int32
    u32 = mybir.dt.uint32
    u8 = mybir.dt.uint8
    ALU = mybir.AluOpType
    ACT = mybir.ActivationFunctionType
    AX = mybir.AxisListType

    P = 128
    B, S, D = x.shape
    NK = vals_dram.shape[1]
    H = 16
    DH = D // H
    DC = D // P
    ST = S // P
    NT = B * ST
    TOK = B * S
    E = w_gate.shape[1]
    F = w_in.shape[2]
    FC = F // P
    TOPK = 2
    EPS = 1e-5
    MASKED = -1e30
    EXP_ROOM = 80.0

    ROWS = 32
    RG = P // ROWS
    HR = ROWS // DH
    GH = 4
    NG = H // GH
    QH = P // ROWS

    SLOT = 256
    SS = SLOT // P
    MAXT = TOPK * TOK // SLOT + E
    PAY = D + 4
    NB = TOK // SLOT
    NPAIR = E // 2
    CH = 4
    NC = NT // CH
    CAP = TOK + SLOT
    LOADS = [(0, ST), (ST, 2 * ST), (2 * ST, NT // 2), (NT // 2, NT)]
    HP = FC // 2

    slots_dram = nc.dram_tensor("slot_rows", (E * CAP, PAY), f32, kind="Internal").ap()
    y_dram = nc.dram_tensor("expert_rows", (TOPK * TOK + SLOT, D), f32, kind="Internal").ap()

    with ExitStack() as stack:
        def sb(name, shape, dt=f32):
            return stack.enter_context(nc.sbuf_tensor(name, shape, dt))

        def sem(name):
            return stack.enter_context(nc.semaphore(name))

        def pair_of(make):
            return [make(0), make(1)]

        x_all = sb("x_all", [P, NT, D])
        ident = sb("ident", [P, P])
        scal = sb("scal", [P, 4])
        scal2 = sb("scal2", [P, 4])
        mask_u8 = sb("mask_u8", [NK, B], u8)
        key_bias = sb("key_bias", [NK, B])
        bias_now = pair_of(lambda i: sb(f"bias_now{i}", [NK, 1]))
        shift = sb("shift", [P, 1])
        wo_sb = sb("wo_sb", [P, DC, D])
        wg_sb = sb("wg_sb", [P, DC, E])
        probs_mem = sb("probs_mem", [P, 2 * H * S])
        probs = probs_mem[0:NK, :].rearrange("k (i h q) -> k i h q", i=2, h=H)
        keys = pair_of(lambda i: sb(f"keys{i}", [P, DC, HR, NK]))
        vals = pair_of(lambda i: sb(f"vals{i}", [NK, H, ROWS]))
        xn = pair_of(lambda i: sb(f"xn{i}", [P, ST, D]))
        q_t = pair_of(lambda i: sb(f"q_t{i}", [P, DC, S]))
        bn1 = sb("bn1", [P, ST, 6])
        mv1 = sb("mv1", [P, ST, 2])
        ve1 = sb("ve1", [P, ST])
        rstd1 = sb("rstd1", [P, ST])
        bn2 = sb("bn2", [P, ST, 6])
        mv2 = sb("mv2", [P, ST, 2])
        ve2 = sb("ve2", [P, ST])
        rstd2 = sb("rstd2", [P, ST])
        minus_half = sb("minus_half", [P, ST])
        mixed = sb("mixed", [P, QH, S])
        rsum = sb("rsum", [P, ST, H])
        att = sb("att", [P, ST, D])
        att_t = sb("att_t", [P, DC, S])
        pay = pair_of(lambda i: sb(f"pay{i}", [P, ST, PAY]))
        xn2_t = sb("xn2_t", [P, DC, S])
        lg = sb("lg", [P, ST, E])
        top_v = sb("top_v", [P, ST, 8])
        top_i = sb("top_i", [P, ST, 8], u32)
        idx = sb("idx", [P, TOPK, ST])
        gap = sb("gap", [P, ST])
        egap = sb("egap", [P, ST])
        den = sb("den", [P, ST])
        onehot = sb("onehot", [P, TOPK, ST, E])
        member = sb("member", [P, ST, E])
        base = sb("base", [P, ST, E])
        pos = sb("pos", [P, ST, E])
        picked = sb("picked", [P, TOPK, ST, E])
        slot_f = sb("slot_f", [P, TOPK, ST])
        slot_i = pair_of(lambda i: sb(f"slot_i{i}", [P, TOPK, ST], i32))
        tri = sb("tri", [P, P])
        ones = sb("ones", [P, P])
        tok_id = sb("tok_id", [P, NT])
        e_iota = sb("e_iota", [P, TOPK * ST, E])
        first_row = sb("first_row", [P, E])
        t_iota = sb("t_iota", [P, E, NB])
        filled = sb("filled", [P, E])
        more = sb("more", [P, E, NB])
        n_tiles = sb("n_tiles", [P, E])
        n_scan = sb("n_scan", [P, E])
        start = sb("start", [P, E])
        plan = sb("plan", [1, 3 * E + 1], i32)
        TOTAL = 3 * E
        w_in_sb = pair_of(lambda i: sb(f"w_in_sb{i}", [P, DC, F]))
        w_out_sb = pair_of(lambda i: sb(f"w_out_sb{i}", [P, FC, D]))
        b_in_sb = sb("b_in_sb", [P, E, FC])
        b_in_now = sb("b_in_now", [P, FC])
        b_out_sb = sb("b_out_sb", [P, E, D])
        pad = sb("pad", [P, SS, PAY])
        xs = sb("xs", [P, SS, PAY])
        tail = sb("tail", [P, SS, PAY - D])
        xs_t = sb("xs_t", [P, DC, SLOT])
        hid = sb("hid", [P, FC, SLOT])
        second = sb("second", [P, SS])
        wdiff = sb("wdiff", [P, SS])
        wgt = sb("wgt", [P, SS])
        dest_f = sb("dest_f", [P, SS])
        dest_i = sb("dest_i", [P, SS], i32)
        y_sb = sb("y_sb", [P, SS, D])

        bank = stack.enter_context(nc.psum_tensor("bank", [P, 8, 512], f32))
        SC = bank[:, 0:4, :]
        TQ = bank[:, 4, :]
        AT = bank[:, 5, :]
        AV = bank[:, 6:8, :]
        HB = [bank[:, i, :] for i in range(HP)]
        XT = bank[:, 4, :]
        YB = [bank[:, 6 + s, :] for s in range(SS)]

        def sems(*names):
            return [sem(n) for n in names]

        x_in = [sem(f"x_in{c}") for c in range(len(LOADS))]
        scal_in, mask_in, wo_in, wg_in, bias_in = sems("scal_in", "mask_in", "wo_in", "wg_in", "bias_in")
        keys_in = pair_of(lambda i: sem(f"keys_in{i}"))
        vals_in = pair_of(lambda i: sem(f"vals_in{i}"))
        ident_done, consts_done, pool_step, base_ready, pad_done = sems(
            "ident_done", "consts_done", "pool_step", "base_ready", "pad_done")
        scal_done, c_done, shift_done, bias_done = sems("scal_done", "c_done", "shift_done", "bias_done")
        bn1_done, mv1_done, ve1_done, rstd1_done, xn_done, tq_done, qt_done = sems(
            "bn1_done", "mv1_done", "ve1_done", "rstd1_done", "xn_done", "tq_done", "qt_done")
        sc_done, tanh_done, exp_done, av_done, mixed_done, tu_done, rsum_done, att_done = sems(
            "sc_done", "tanh_done", "exp_done", "av_done", "mixed_done", "tu_done", "rsum_done", "att_done")
        ta_done, att_t_done, proj_done, x2_done, bn2_done, mv2_done, ve2_done, rstd2_done, xn2_done = sems(
            "ta_done", "att_t_done", "proj_done", "x2_done", "bn2_done", "mv2_done", "ve2_done", "rstd2_done",
            "xn2_done")
        t2_done, xn2_t_done, gate_done, lg_done, topv_done, topi_done, gap_done, egap_done = sems(
            "t2_done", "xn2_t_done", "gate_done", "lg_done", "topv_done", "topi_done", "gap_done", "egap_done")
        idx_done, w_done = sems("idx_done", "w_done")
        onehot_done, member_done, rank_done, base_done, rank_read, pos_done, picked_done, den_done = sems(
            "onehot_done", "member_done", "rank_done", "base_done", "rank_read", "pos_done", "picked_done",
            "den_done")
        slot_done, slots_done, route_step, plan_done, pad_out = sems(
            "slot_done", "slots_done", "route_step", "plan_done", "pad_out")
        sent = pair_of(lambda i: sem(f"sent{i}"))
        w_in_in = pair_of(lambda i: sem(f"w_in_in{i}"))
        w_out_in = pair_of(lambda i: sem(f"w_out_in{i}"))
        b_in_done, xs_in, xs_free, tx_done, xs_t_done, h_done, gelu_done, y_done, y_sb_done = sems(
            "b_in_done", "xs_in", "xs_free", "tx_done", "xs_t_done", "h_done", "gelu_done", "y_done", "y_sb_done")
        meta_step, yb_read, y_sent, y_free = sems("meta_step", "yb_read", "y_sent", "y_free")
        sum_in = [sem(f"sum_in{c}") for c in range(NC)]
        half_done, sum_done, out_sent = sems("half_done", "sum_done", "out_sent")

        x_view = x.rearrange("b (s p) d -> p (b s) d", p=P)
        out_view = out.rearrange("b (s p) d -> p (b s) d", p=P)
        slots_view = slots_dram.rearrange("(e t s p) w -> e t p s w", e=E, s=SS, p=P)
        y_view = y_dram[0:TOPK * TOK, :].rearrange("(k t p) d -> p k t d", k=TOPK, p=P)
        w_in_view = w_in.rearrange("e (c p) f -> e p c f", p=P)
        w_out_view = w_out.rearrange("e (c p) d -> e p c d", p=P)
        sum_buf = probs_mem[:, :].rearrange("p (c k t d) -> p c k t d", c=NC, k=TOPK, t=CH)

        def value(eng, v):
            return v if type(v) is int else eng.to_reg(v)

        def later(b, n):
            return type(b) is not int or b >= n

        block = stack.enter_context(nc.Block())

        @block.sync
        def _(sp):
            def load_x(c):
                t0, t1 = LOADS[c]
                sp.dma_start(x_all[:, t0:t1, :], x_view[:, t0:t1, :]).then_inc(x_in[c], 16)

            def load_keys(b, i):
                if later(b, 2):
                    sp.wait_ge(sc_done, (b - 1) * NG)
                sp.dma_start(keys[i][:, :, :, :], keys_dram[b]).then_inc(keys_in[i], 16)

            def load_vals(b, i):
                if later(b, 2):
                    sp.wait_ge(av_done, b - 1)
                sp.dma_start(vals[i][:, :, :], vals_dram[b]).then_inc(vals_in[i], 16)

            load_x(0)
            load_keys(0, 0)
            load_x(1)
            load_keys(1, 1)
            load_vals(0, 0)
            load_vals(1, 1)
            for c in range(2, len(LOADS)):
                load_x(c)
            with sp.Fori(0, (B - 2) // 2) as i:
                load_keys(2 * i + 2, 0)
                load_vals(2 * i + 2, 0)
                load_keys(2 * i + 3, 1)
                load_vals(2 * i + 3, 1)
            sp.wait_ge(pad_done, 4)
            sp.wait_ge(plan_done, 1)
            for e in range(E):
                row = sp.value_load(plan[0:1, 2 * E + e:2 * E + e + 1], min_val=e * CAP, max_val=e * CAP + TOK)
                sp.dma_start(slots_dram[bass.ds(row, SLOT), :].rearrange("(s p) w -> p s w", p=P), pad[:, :, :]
                             ).then_inc(pad_out, 16)
            sp.wait_ge(pad_out, 16 * E)
            for i in range(2):
                sp.wait_ge(sent[i], 16 * TOPK * NT // 2)

            def load_slots(e):
                first = sp.value_load(plan[0:1, bass.ds(e, 1)], min_val=0, max_val=MAXT)
                count = sp.value_load(plan[0:1, bass.ds(e + E, 1)], min_val=1, max_val=NB)
                with sp.Fori(0, count) as t:
                    sp.wait_ge(xs_free, first + t + 1)
                    sp.dma_start(xs[:, :, :], slots_view[e, t]).then_inc(xs_in, 16)

            with sp.Fori(0, E) as e:
                load_slots(e)
            total = sp.value_load(plan[0:1, TOTAL:TOTAL + 1], min_val=E, max_val=MAXT)
            sp.wait_ge(xs_free, total + 1)
            sp.dma_start(xs[:, :, :], slots_view[0, 0]).then_inc(xs_in, 16)
            sp.wait_ge(y_sent, total * (16 * SS))
            for c in range(NC):
                for k in range(TOPK):
                    sp.dma_start(sum_buf[:, c, k, :, :], y_view[:, k, c * CH:(c + 1) * CH, :]
                                 ).then_inc(sum_in[c], 16)

        @block.gpsimd
        def _(pool):
            pool.memset(minus_half[:, :], -0.5).then_inc(pool_step, 1)
            pool.memset(ident[:, :], 0.0).then_inc(pool_step, 1)
            pool.wait_ge(pool_step, 2)
            pool.affine_select(out=ident[:, :], in_=ident[:, :], compare_op=ALU.not_equal, fill=1.0, base=0,
                               pattern=[[-1, P]], channel_multiplier=1).then_inc(ident_done, 1)

            def rstd(b, mv, ve, done_in, ve_done, r, done_out):
                after = value(pool, b + 1)
                pool.wait_ge(ident_done, 1)
                pool.wait_ge(done_in, after)
                pool.tensor_scalar(ve[:, :], mv[:, :, 1], EPS, None, ALU.add).then_inc(ve_done, 1)
                pool.wait_ge(ve_done, b + 1)
                pool.tensor_tensor(r[:, :], ve[:, :], minus_half[:, :], ALU.pow).then_inc(done_out, 1)

            def step(b, i, front=True, mid=True, late=True):
                if front:
                    rstd(b + 1, mv1, ve1, mv1_done, ve1_done, rstd1, rstd1_done)
                if mid:
                    rstd(b - 1, mv2, ve2, mv2_done, ve2_done, rstd2, rstd2_done)
                if late:
                    send(b - 2, i)

            def send(b, i):
                after = value(pool, b + 1)
                pool.wait_ge(ident_done, 1)
                pool.wait_ge(slots_done, after)
                for k in range(TOPK):
                    for s in range(ST):
                        pool.indirect_dma_start(
                            out=slots_dram,
                            out_offset=bass.IndirectOffsetOnAxis(ap=slot_i[i][:, k, s:s + 1], axis=0),
                            in_=pay[i][:, s, :], in_offset=None).then_inc(sent[i], 16)

            rstd(0, mv1, ve1, mv1_done, ve1_done, rstd1, rstd1_done)
            step(0, 0, mid=False, late=False)
            pool.memset(ones[:, :], 1.0).then_inc(pool_step, 1)
            pool.wait_ge(pool_step, 3)
            pool.affine_select(out=tri[:, :], in_=ones[:, :], compare_op=ALU.is_gt, fill=0.0, base=0,
                               pattern=[[1, P]], channel_multiplier=-1)
            iota = dict(base=0, allow_small_or_imprecise_dtypes=True)
            pool.iota(base[:, 0, :], [[CAP, E]], channel_multiplier=0, **iota)
            pool.iota(first_row[:, :], [[CAP, E]], channel_multiplier=0, **iota)
            pool.iota(tok_id[:, :], [[P, NT]], channel_multiplier=1, **iota)
            pool.iota(e_iota[:, :, :], [[0, TOPK * ST], [1, E]], channel_multiplier=0, **iota)
            pool.iota(t_iota[:, :, :], [[0, E], [SLOT, NB]], channel_multiplier=0, **iota
                      ).then_inc(consts_done, 1)
            step(1, 1, late=False)
            pool.memset(pad[:, :, 0:D + 2], 0.0).then_inc(pad_done, 1)
            pool.memset(pad[:, :, D + 2:D + 3], -1.0).then_inc(pad_done, 1)
            for s in range(SS):
                pool.iota(pad[:, s, D + 3:D + 4], [[0, 1]], base=TOK + s * P, channel_multiplier=1,
                          allow_small_or_imprecise_dtypes=True).then_inc(pad_done, 1)
            with pool.Fori(0, (B - 4) // 2) as i:
                step(2 * i + 2, 0)
                step(2 * i + 3, 1)
            step(B - 2, 0)
            step(B - 1, 1, front=False)
            step(B, 0, front=False)
            step(B + 1, 1, front=False, mid=False)
            pool.wait_ge(plan_done, 1)
            total = pool.value_load(plan[0:1, TOTAL:TOTAL + 1], min_val=E, max_val=MAXT)
            pool.nop().then_inc(y_free, 1)
            with pool.Fori(0, total) as t:
                after = value(pool, t + 1)
                pool.wait_ge(plan_done, 1)
                pool.wait_ge(y_sb_done, after)
                for s in range(SS):
                    pool.indirect_dma_start(
                        out=y_dram, out_offset=bass.IndirectOffsetOnAxis(ap=dest_i[:, s:s + 1], axis=0),
                        in_=y_sb[:, s, :], in_offset=None).then_inc(y_sent, 16)
                pool.wait_ge(y_sent, t * (16 * SS) + 16 * SS)
                pool.nop().then_inc(y_free, 1)

        @block.scalar
        def _(act):
            act.dma_start(scal[:, :], scalars.partition_broadcast(P)).then_inc(scal_in, 16)
            act.dma_start(mask_u8[:, :], mask_cols).then_inc(mask_in, 16)
            act.wait_ge(scal_in, 16)
            act.activation(scal2[:, 2:4], scal[:, 2:4], ACT.Tanh).then_inc(scal_done, 1)
            act.activation(scal2[:, 0:1], scal[:, 0:1], ACT.Copy, scale=float(DH) ** -0.5
                           ).then_inc(scal_done, 1)
            act.activation(scal2[:, 1:2], scal[:, 1:2], ACT.Exp).then_inc(c_done, 1)
            act.wait_ge(scal_done, 2)
            act.wait_ge(c_done, 1)

            def soften(b, i):
                for g in range(NG):
                    if g == 0 and later(b, 2):
                        act.wait_ge(av_done, b - 1)
                    act.wait_ge(sc_done, b * NG + (g + 1))
                    r0 = GH // HR * (g % 2)
                    act.activation(probs[:, i, g * GH:(g + 1) * GH, :],
                                   SC[0:NK, r0:r0 + GH // HR, :].rearrange("k r (h q) -> k (r h) q", q=S),
                                   ACT.Tanh, scale=scal2[0:NK, 0:1]).then_inc(tanh_done, 1)
                    if g % 2:
                        act.wait_ge(bias_done, b + 1)
                        act.wait_ge(tanh_done, b * NG + (g + 1))
                        both = probs[:, i, (g - 1) * GH:(g + 1) * GH, :]
                        act.activation(both, both, ACT.Exp, bias=bias_now[i][:, :],
                                       scale=scal2[0:NK, 1:2]).then_inc(exp_done, 1)

            def choice(b):
                act.wait_ge(gap_done, b + 1)
                act.activation(egap[:, :], gap[:, :], ACT.Exp).then_inc(egap_done, 1)

            soften(0, 0)
            act.dma_start(wo_sb[:, :, :], wo_t.rearrange("(c p) f -> p c f", p=P)).then_inc(wo_in, 16)
            act.dma_start(wg_sb[:, :, :], w_gate.rearrange("(c p) e -> p c e", p=P)).then_inc(wg_in, 16)
            soften(1, 1)
            for e in range(2):
                act.dma_start(w_in_sb[e][:, :, :], w_in_view[e]).then_inc(w_in_in[e], 16)
                act.dma_start(w_out_sb[e][:, :, :], w_out_view[e]).then_inc(w_out_in[e], 16)
            act.dma_start(b_in_sb[:, :, :], b_in).then_inc(bias_in, 16)
            act.dma_start(b_out_sb[:, :, :], b_out.partition_broadcast(P)).then_inc(bias_in, 16)
            with act.Fori(0, (B - 2) // 2) as i:
                soften(2 * i + 2, 0)
                choice(2 * i)
                soften(2 * i + 3, 1)
                choice(2 * i + 1)
            choice(B - 2)
            choice(B - 1)

            def next_weights(e, i, after):
                act.wait_ge(y_done, after)
                act.dma_start(w_in_sb[i][:, :, :], w_in_view[e + 2]).then_inc(w_in_in[i], 16)
                act.dma_start(w_out_sb[i][:, :, :], w_out_view[e + 2]).then_inc(w_out_in[i], 16)

            def expert(e):
                first = act.value_load(plan[0:1, bass.ds(e, 1)], min_val=0, max_val=MAXT)
                count = act.value_load(plan[0:1, bass.ds(e + E, 1)], min_val=1, max_val=NB)
                act.wait_ge(b_in_done, e + 1)
                with act.Fori(0, count) as t:
                    for m in range(FC):
                        if m % 2 == 0:
                            act.wait_ge(h_done, (first + t) * HP + (m // 2 + 1))
                        ins = act.activation(hid[:, m, :], HB[m // 2][:, (m % 2) * SLOT:(m % 2 + 1) * SLOT],
                                             ACT.Gelu, bias=b_in_now[:, m:m + 1])
                        if m % 2:
                            ins.then_inc(gelu_done, 1)
                return first + count

            act.wait_ge(plan_done, 1)
            with act.Fori(0, NPAIR - 1) as i:
                next_weights(2 * i, 0, expert(2 * i))
                next_weights(2 * i + 1, 1, expert(2 * i + 1))
            expert(E - 2)
            expert(E - 1)
            for c in range(NC):
                act.wait_ge(sum_done, c + 1)
                act.dma_start(out_view[:, c * CH:(c + 1) * CH, :], sum_buf[:, c, 0, :, :]).then_inc(out_sent, 16)
            act.wait_ge(out_sent, 16 * NC)

        @block.vector
        def _(dve):
            def rows(b, s):
                return x_all[:, bass.ds(b * ST + s, 1), :].squeeze(1)

            def stats(b, bn, mv, bnd, mvd):
                after = value(dve, b + 1)
                dve.wait_ge(x_in[0], 16)
                if bnd is bn2_done:
                    dve.wait_ge(x2_done, after)
                for s in range(ST):
                    ins = dve.bn_stats(bn[:, s, :], rows(b, s))
                ins.then_inc(bnd, 1)
                dve.wait_ge(x_in[0], 16)
                dve.wait_ge(bnd, after)
                for s in range(ST):
                    ins = dve.bn_aggr(mv[:, s, :], bn[:, s, :])
                ins.then_inc(mvd, 1)

            def stats1(b):
                stats(b, bn1, mv1, bn1_done, mv1_done)

            def norm1(b, i):
                dve.wait_ge(rstd1_done, b + 1)
                for s in range(ST):
                    ins = dve.tensor_scalar(xn[i][:, s, :], rows(b, s), mv1[:, s, 0:1], rstd1[:, s:s + 1],
                                            ALU.subtract, ALU.mult)
                ins.then_inc(xn_done, 1)

            def query(b, i):
                dve.wait_ge(tq_done, b + 1)
                dve.tensor_copy(q_t[i][:, :, :], TQ.rearrange("p (c q) -> p c q", c=DC)).then_inc(qt_done, 1)
                dve.tensor_copy(bias_now[i][:, :], key_bias[:, bass.ds(b, 1)]).then_inc(bias_done, 1)

            def mixed_out(b):
                dve.wait_ge(av_done, b + 1)
                dve.tensor_copy(mixed[:, :, :].rearrange("p (s g) q -> p s (g q)", s=ST), AV).then_inc(mixed_done, 1)

            def attend(b):
                dve.wait_ge(tu_done, b + 1)
                turned_v = AV.rearrange("p s (h w) -> p s h w", w=ROWS)
                dve.reciprocal(rsum[:, :, :], turned_v[:, :, :, DH]).then_inc(rsum_done, 1)
                dve.wait_ge(rsum_done, b + 1)
                for s in range(ST):
                    ins = dve.tensor_tensor(att[:, s, :].rearrange("p (h d) -> p h d", h=H),
                                            turned_v[:, s, :, 0:DH],
                                            rsum[:, s, :].unsqueeze(2).to_broadcast([P, H, DH]), ALU.mult)
                ins.then_inc(att_done, 1)

            def att_turned(b):
                dve.wait_ge(ta_done, b + 1)
                dve.tensor_copy(att_t[:, :, :], AT.rearrange("p (c q) -> p c q", c=DC)).then_inc(att_t_done, 1)

            def residual(b):
                dve.wait_ge(proj_done, b + 1)
                for s in range(ST):
                    ins = dve.scalar_tensor_tensor(rows(b, s), AT[:, s * D:(s + 1) * D], scal2[:, 2:3], rows(b, s),
                                                   ALU.mult, ALU.add)
                ins.then_inc(x2_done, 1)
                stats(b, bn2, mv2, bn2_done, mv2_done)

            def norm2(b, i, n):
                if later(b, 2):
                    dve.wait_ge(sent[i], n * (16 * TOPK * ST))
                dve.wait_ge(rstd2_done, b + 1)
                for s in range(ST):
                    ins = dve.tensor_scalar(pay[i][:, s, 0:D], rows(b, s), mv2[:, s, 0:1], rstd2[:, s:s + 1],
                                            ALU.subtract, ALU.mult)
                ins.then_inc(xn2_done, 1)

            def xn2_turned(b):
                dve.wait_ge(t2_done, b + 1)
                dve.tensor_copy(xn2_t[:, :, :], TQ.rearrange("p (c q) -> p c q", c=DC)).then_inc(xn2_t_done, 1)

            def choose(b):
                dve.wait_ge(gate_done, b + 1)
                dve.tensor_copy(lg[:, :, :], TQ[:, 0:ST * E].rearrange("p (s e) -> p s e", s=ST)).then_inc(lg_done, 1)
                after = value(dve, b + 1)
                dve.wait_ge(x_in[0], 16)
                dve.wait_ge(lg_done, after)
                for s in range(ST):
                    ins = dve.max(top_v[:, s, :], lg[:, s, :])
                ins.then_inc(topv_done, 1)
                dve.wait_ge(x_in[0], 16)
                dve.wait_ge(topv_done, after)
                for s in range(ST):
                    ins = dve.max_index(top_i[:, s, :], top_v[:, s, :], lg[:, s, :])
                ins.then_inc(topi_done, 1)
                dve.tensor_tensor(gap[:, :], top_v[:, :, 1], top_v[:, :, 0], ALU.subtract).then_inc(gap_done, 1)
                dve.wait_ge(topi_done, after)
                dve.tensor_copy(idx[:, :, :].rearrange("p k s -> p s k"), top_i[:, :, 0:TOPK]).then_inc(idx_done, 1)
                dve.wait_ge(idx_done, after)
                dve.tensor_tensor(onehot[:, :, :, :].rearrange("p k s e -> p (k s) e"),
                                  idx[:, :, :].rearrange("p k s -> p (k s)").unsqueeze(2).to_broadcast([P, TOPK * ST, E]),
                                  e_iota[:, :, :], ALU.is_equal).then_inc(onehot_done, 1)
                dve.wait_ge(onehot_done, after)
                dve.tensor_tensor(member[:, :, :], onehot[:, 0, :, :], onehot[:, 1, :, :], ALU.add
                                  ).then_inc(member_done, 1)

            def slots(b, i):
                dve.wait_ge(egap_done, b + 1)
                dve.tensor_scalar(den[:, :], egap[:, :], 1.0, None, ALU.add).then_inc(den_done, 1)
                after = value(dve, b + 1)
                dve.wait_ge(rank_done, after)
                in_tile = TQ[:, 0:ST * E].rearrange("p (s e) -> p s e", s=ST)
                of_tile = TQ[:, ST * E:2 * ST * E].rearrange("p (s e) -> p s e", s=ST)
                dve.tensor_tensor(base[:, 1, :], base[:, 0, :], of_tile[:, 0, :], ALU.add).then_inc(base_done, 1)
                dve.wait_ge(den_done, 2 * b + 1)
                dve.reciprocal(den[:, :], den[:, :]).then_inc(den_done, 1)
                dve.wait_ge(base_done, b + 1)
                dve.tensor_tensor(pos[:, :, :], in_tile, base[:, :, :], ALU.add).then_inc(pos_done, 1)
                dve.wait_ge(den_done, 2 * b + 2)
                dve.tensor_scalar(pay[i][:, :, D], den[:, :], scal2[:, 3:4], None, ALU.mult).then_inc(w_done, 1)
                dve.wait_ge(pos_done, after)
                dve.tensor_tensor(base[:, 0, :], base[:, 1, :], of_tile[:, 1, :], ALU.add).then_inc(rank_read, 1)
                dve.tensor_tensor(picked[:, :, :, :].rearrange("p k s e -> p k (s e)"),
                                  onehot[:, :, :, :].rearrange("p k s e -> p k (s e)"),
                                  pos[:, :, :].rearrange("p s e -> p (s e)").unsqueeze(1).to_broadcast([P, TOPK, ST * E]),
                                  ALU.mult).then_inc(picked_done, 1)
                dve.wait_ge(w_done, after)
                dve.tensor_tensor(pay[i][:, :, D + 1], pay[i][:, :, D], egap[:, :], ALU.mult)
                dve.wait_ge(picked_done, after)
                dve.tensor_reduce(slot_f[:, :, :].rearrange("p k s -> p (k s)"),
                                  picked[:, :, :, :].rearrange("p k s e -> p (k s) e"), axis=AX.X, op=ALU.add
                                  ).then_inc(slot_done, 1)
                dve.tensor_copy(pay[i][:, :, D + 2], idx[:, 0, :])
                dve.tensor_copy(pay[i][:, :, D + 3], tok_id[:, bass.ds(b * ST, ST)])
                dve.wait_ge(slot_done, after)
                dve.tensor_copy(slot_i[i][:, :, :], slot_f[:, :, :]).then_inc(slots_done, 1)

            dve.wait_ge(x_in[0], 16)
            stats1(0)
            dve.wait_ge(c_done, 1)
            dve.tensor_scalar(shift[:, :], scal2[:, 1:2], -1.0, EXP_ROOM, ALU.mult, ALU.add
                              ).then_inc(shift_done, 1)
            dve.wait_ge(shift_done, 1)
            dve.tensor_scalar(shift[:, :], shift[:, :], 0.0, None, ALU.min).then_inc(shift_done, 1)
            dve.wait_ge(shift_done, 2)
            dve.wait_ge(mask_in, 16)
            dve.tensor_scalar(key_bias[:, :], mask_u8[:, :], MASKED, shift[0:NK, :], ALU.mult, ALU.add
                              ).then_inc(shift_done, 1)
            dve.wait_ge(shift_done, 3)
            norm1(0, 0)
            dve.memset(tail[:, :, :], 0.0).then_inc(xs_free, 1)
            dve.memset(wgt[:, :], 0.0).then_inc(yb_read, 1)

            def step(b, i, n, front=True, query_too=True, mid=True, late=True):
                if query_too:
                    query(b, i)
                if front:
                    stats1(b + 1)
                    norm1(b + 1, 1 - i)
                if mid:
                    mixed_out(b - 1)
                if late:
                    xn2_turned(b - 2)
                if mid:
                    attend(b - 1)
                if late:
                    choose(b - 2)
                if mid:
                    att_turned(b - 1)
                    residual(b - 1)
                if late:
                    slots(b - 2, i)
                if mid:
                    norm2(b - 1, 1 - i, n if i else n - 1)

            dve.wait_ge(x_in[1], 16)
            step(0, 0, 0, mid=False, late=False)
            for c in range(2, len(LOADS)):
                dve.wait_ge(x_in[c], 16)
            dve.wait_ge(scal_done, 2)
            step(1, 1, 0, late=False)
            dve.wait_ge(consts_done, 1)
            with dve.Fori(0, (B - 4) // 2) as i:
                step(2 * i + 2, 0, i + 1)
                step(2 * i + 3, 1, i + 1)
            step(B - 2, 0, B // 2 - 1)
            step(B - 1, 1, B // 2 - 1, front=False)
            step(B, 0, B // 2, front=False, query_too=False)
            step(B + 1, 1, B // 2, front=False, query_too=False, mid=False)

            count = [0]

            def link(ins):
                count[0] += 1
                ins.then_inc(route_step, 1)
                dve.wait_ge(route_step, count[0])

            dve.wait_ge(rank_read, B)
            link(dve.tensor_tensor(filled[:, :], base[:, 0, :], first_row[:, :], ALU.subtract))
            link(dve.tensor_tensor(more[:, :, :], filled[:, :].unsqueeze(2).to_broadcast([P, E, NB]),
                                   t_iota[:, :, :], ALU.is_gt))
            link(dve.tensor_reduce(n_tiles[:, :], more[:, :, :], axis=AX.X, op=ALU.add))
            link(dve.tensor_scalar(n_tiles[:, :], n_tiles[:, :], 1.0, None, ALU.max))
            link(dve.tensor_tensor_scan(n_scan[:, :], ones[:, 0:E], n_tiles[:, :], 0.0, ALU.mult, ALU.add))
            link(dve.tensor_tensor(start[:, :], n_scan[:, :], n_tiles[:, :], ALU.subtract))
            dve.tensor_copy(plan[0:1, 0:E], start[0:1, :])
            dve.tensor_copy(plan[0:1, E:2 * E], n_tiles[0:1, :])
            dve.tensor_copy(plan[0:1, 2 * E:3 * E], base[0:1, 0, :])
            dve.tensor_copy(plan[0:1, TOTAL:TOTAL + 1], n_scan[0:1, E - 1:E]).then_inc(plan_done, 1)

            def turned(t):
                dve.wait_ge(tx_done, t + 1)
                dve.tensor_copy(xs_t[:, :, :], XT.rearrange("p (c q) -> p c q", c=DC)).then_inc(xs_t_done, 1)
                if later(t, 1):
                    dve.wait_ge(meta_step, 5 * t)
                dve.tensor_copy(tail[:, :, :], xs[:, :, D:PAY]).then_inc(xs_free, 1)

            def meta(e, t):
                dve.wait_ge(xs_free, t + 2)
                dve.tensor_scalar(second[:, :], tail[:, :, 2], e_iota[:, 0, bass.ds(e, 1)], None, ALU.not_equal
                                  ).then_inc(meta_step, 1)
                dve.tensor_tensor(wdiff[:, :], tail[:, :, 1], tail[:, :, 0], ALU.subtract).then_inc(meta_step, 1)
                dve.wait_ge(meta_step, 5 * t + 2)
                dve.tensor_tensor(wdiff[:, :], wdiff[:, :], second[:, :], ALU.mult).then_inc(meta_step, 1)
                dve.scalar_tensor_tensor(dest_f[:, :], second[:, :], float(TOK), tail[:, :, 3], ALU.mult, ALU.add
                                         ).then_inc(meta_step, 1)
                dve.wait_ge(meta_step, 5 * t + 4)
                dve.tensor_tensor(wgt[:, :], wdiff[:, :], tail[:, :, 0], ALU.add).then_inc(meta_step, 1)

            def expert(e):
                first = dve.value_load(plan[0:1, bass.ds(e, 1)], min_val=0, max_val=MAXT)
                count_e = dve.value_load(plan[0:1, bass.ds(e + E, 1)], min_val=1, max_val=NB)
                dve.tensor_copy(b_in_now[:, :], b_in_sb[:, bass.ds(e, 1), :].squeeze(1)).then_inc(b_in_done, 1)
                with dve.Fori(0, count_e) as t0:
                    t = dve.snap(first + t0)
                    meta(e, t)
                    turned(t + 1)
                    dve.wait_ge(y_done, t + 1)
                    dve.wait_ge(y_free, t + 1)
                    for s in range(SS):
                        ins = dve.tensor_tensor(y_sb[:, s, :], YB[s][:, 0:D], b_out_sb[:, bass.ds(e, 1), :].squeeze(1),
                                                ALU.add)
                    ins.then_inc(yb_read, 1)
                    dve.tensor_copy(dest_i[:, :], dest_f[:, :])
                    dve.wait_ge(yb_read, t + 2)
                    for s in range(SS):
                        ins = dve.tensor_scalar(y_sb[:, s, :], y_sb[:, s, :], wgt[:, s:s + 1], None, ALU.mult)
                    ins.then_inc(y_sb_done, 1)

            turned(0)
            dve.wait_ge(bias_in, 32)
            with dve.Fori(0, E) as e:
                expert(e)
            for c in range(NC):
                dve.wait_ge(sum_in[c], 16 * TOPK)
                a, b2 = sum_buf[:, c, 0, :, :], sum_buf[:, c, 1, :, :]
                dve.tensor_tensor(a, a, b2, ALU.add).then_inc(half_done, 1)
                dve.wait_ge(half_done, c + 1)
                dve.tensor_tensor(a, a, x_all[:, c * CH:(c + 1) * CH, :], ALU.add).then_inc(sum_done, 1)

        @block.tensor
        def _(pe):
            def turn(dst, src):
                for s in range(ST):
                    for c in range(DC):
                        ins = pe.transpose(dst[:, c * S + s * P:c * S + (s + 1) * P], src[:, s, c * P:(c + 1) * P],
                                           ident[:, :])
                return ins

            def turn_queries(b, i):
                pe.wait_ge(xn_done, b + 1)
                if later(b, 3):
                    pe.wait_ge(rank_read, b - 2)
                elif b > 0:
                    pe.wait_ge(qt_done, b)
                turn(TQ, xn[i]).then_inc(tq_done, 1)

            def scores(b, i, g, n):
                if g == 0:
                    pe.wait_ge(qt_done, b + 1)
                    pe.wait_ge(keys_in[i], (n + 1) * 16)
                if later(b, 1) or g >= 2:
                    pe.wait_ge(tanh_done, b * NG + (g - 1))
                c = g // 2
                for hr in range(HR):
                    for r in range(GH // HR):
                        rg = GH // HR * (g % 2) + r
                        rows = slice(rg * ROWS, (rg + 1) * ROWS)
                        ins = pe.matmul(SC[0:NK, rg, hr * S:(hr + 1) * S], keys[i][rows, c, hr, :], q_t[i][rows, c, :],
                                        start=True, stop=True)
                ins.then_inc(sc_done, 1)

            def values(b, i, half, n):
                pe.wait_ge(exp_done, 2 * b + (half + 1))
                if half == 0:
                    pe.wait_ge(vals_in[i], (n + 1) * 16)
                    if later(b, 1):
                        pe.wait_ge(att_done, b)
                for h in range(half * H // 2, (half + 1) * H // 2):
                    g, j = h // QH, h % QH
                    ins = pe.matmul(AV[j * ROWS:(j + 1) * ROWS, g // 2, (g % 2) * S:(g % 2 + 1) * S],
                                    vals[i][:, h, :], probs[:, i, h, :], start=True, stop=True)
                if half:
                    ins.then_inc(av_done, 1)

            def turn_mixed(b):
                pe.wait_ge(mixed_done, b + 1)
                for s in range(ST):
                    for g in range(QH):
                        ins = pe.transpose(AV[:, s, g * P:(g + 1) * P], mixed[:, g, s * P:(s + 1) * P], ident[:, :])
                ins.then_inc(tu_done, 1)

            def turn_att(b):
                pe.wait_ge(att_done, b + 1)
                if later(b, 1):
                    pe.wait_ge(x2_done, b)
                turn(AT, att).then_inc(ta_done, 1)

            def project(b):
                pe.wait_ge(att_t_done, b + 1)
                for s in range(ST):
                    for c in range(DC):
                        ins = pe.matmul(AT[:, s * D:(s + 1) * D], att_t[:, c, s * P:(s + 1) * P], wo_sb[:, c, :],
                                        start=(c == 0), stop=(c == DC - 1))
                ins.then_inc(proj_done, 1)

            def turn_xn2(b, i):
                pe.wait_ge(xn2_done, b + 1)
                turn(TQ, pay[i]).then_inc(t2_done, 1)

            def gate(b):
                pe.wait_ge(xn2_t_done, b + 1)
                for s in range(ST):
                    for c in range(DC):
                        ins = pe.matmul(TQ[:, s * E:(s + 1) * E], xn2_t[:, c, s * P:(s + 1) * P], wg_sb[:, c, :],
                                        start=(c == 0), stop=(c == DC - 1))
                ins.then_inc(gate_done, 1)

            def rank(b):
                pe.wait_ge(member_done, b + 1)
                flat = member[:, :, :].rearrange("p s e -> p (s e)")
                pe.matmul(TQ[:, 0:ST * E], tri[:, :], flat, start=True, stop=True)
                pe.matmul(TQ[:, ST * E:2 * ST * E], ones[:, :], flat, start=True, stop=True).then_inc(rank_done, 1)

            def step(b, i, n, front=True, mid=True, late=True):
                n_mid = n if i else n - 1
                if mid:
                    values(b - 1, 1 - i, 0, n_mid)
                if front:
                    turn_queries(b, i)
                if mid:
                    values(b - 1, 1 - i, 1, n_mid)
                if front:
                    scores(b, i, 0, n)
                if late:
                    turn_xn2(b - 2, i)
                if front:
                    scores(b, i, 1, n)
                if mid:
                    turn_mixed(b - 1)
                if late:
                    gate(b - 2)
                if front:
                    scores(b, i, 2, n)
                if mid:
                    turn_att(b - 1)
                if front:
                    scores(b, i, 3, n)
                if mid:
                    project(b - 1)
                if late:
                    rank(b - 2)

            pe.wait_ge(ident_done, 1)
            step(0, 0, 0, mid=False, late=False)
            pe.wait_ge(wo_in, 16)
            pe.wait_ge(wg_in, 16)
            step(1, 1, 0, late=False)
            pe.wait_ge(consts_done, 1)
            step(2, 0, 1)
            step(3, 1, 1)
            with pe.Fori(0, (B - 4) // 2) as i:
                step(2 * i + 4, 0, i + 2)
                step(2 * i + 5, 1, i + 2)
            pe.wait_ge(qt_done, B)
            pe.wait_ge(rank_read, B - 2)
            step(B, 0, B // 2, front=False)
            pe.wait_ge(rank_read, B - 1)
            step(B + 1, 1, B // 2, front=False, mid=False)

            def turn_slots(t):
                pe.wait_ge(xs_in, (t + 1) * 16)
                turn(XT, xs).then_inc(tx_done, 1)

            def expert(e, i, pair):
                first = pe.value_load(plan[0:1, bass.ds(e, 1)], min_val=0, max_val=MAXT)
                count = pe.value_load(plan[0:1, bass.ds(e + E, 1)], min_val=1, max_val=NB)
                loads = value(pe, (pair + 1) * 16)
                pe.wait_ge(plan_done, 1)
                pe.wait_ge(w_in_in[i], loads)
                pe.wait_ge(w_out_in[i], loads)
                with pe.Fori(0, count) as t0:
                    t = pe.snap(first + t0)
                    pe.wait_ge(xs_t_done, t + 1)
                    for m in range(FC):
                        for c in range(DC):
                            ins = pe.matmul(HB[m // 2][:, (m % 2) * SLOT:(m % 2 + 1) * SLOT],
                                            w_in_sb[i][:, c, m * P:(m + 1) * P], xs_t[:, c, :],
                                            start=(c == 0), stop=(c == DC - 1))
                        if m % 2:
                            ins.then_inc(h_done, 1)
                    turn_slots(t + 1)
                    pe.wait_ge(yb_read, t + 1)
                    for m in range(FC):
                        if m % 2 == 0:
                            pe.wait_ge(gelu_done, t * HP + (m // 2 + 1))
                        for s in range(SS):
                            ins = pe.matmul(YB[s][:, 0:D], hid[:, m, s * P:(s + 1) * P], w_out_sb[i][:, m, :],
                                            start=(m == 0), stop=(m == FC - 1))
                    ins.then_inc(y_done, 1)

            pe.wait_ge(rank_read, B)
            turn_slots(0)
            pe.wait_ge(plan_done, 1)
            with pe.Fori(0, NPAIR) as i:
                expert(2 * i, 0, i)
                expert(2 * i + 1, 1, i)


_OUT = (8, 256, 256)


def kernel(**inputs):
    import numpy as np
    import concourse.bacc as bacc
    from concourse.bass_utils import run_bass_kernel_spmd

    a = {k: np.asarray(v) for k, v in inputs.items()}
    ctx = a["ctx_1024"]
    b, nk, d = ctx.shape
    h, dh, p = 16, d // 16, 128
    by_head = ctx.transpose(0, 2, 1).reshape(b, d // p, p // (2 * dh), 2, dh, nk)
    keys = np.zeros((b, p // (2 * dh), 2, dh, d // p, 2, nk), ctx.dtype)
    for hr in range(2):
        keys[:, :, hr, :, :, hr, :] = by_head[:, :, :, hr].transpose(0, 2, 3, 1, 4)
    vals = np.ones((b, nk, h, 2 * dh), ctx.dtype)
    vals[..., :dh] = ctx.reshape(b, nk, h, dh)
    b_in = a["L0_ffn_b_in"]
    laid_out = {
        "x": a["x"],
        "keys_dram": keys.reshape(b, p, d // p, 2, nk),
        "vals_dram": vals,
        "mask_cols": np.ascontiguousarray(a["mask_Bx1xS2_bk0"][:, 0, :].T),
        "scalars": np.concatenate([a[n].reshape(1) for n in ("L0_xattn_scale", "L0_xattn_log_C", "g_xattn", "g_ffn")]),
        "wo_t": np.ascontiguousarray(a["L0_xattn_W_out"].T),
        "w_gate": a["L0_ffn_W_gate"],
        "w_in": a["L0_ffn_W_in"],
        "b_in": np.ascontiguousarray(b_in.reshape(b_in.shape[0], -1, p).transpose(2, 0, 1)),
        "w_out": a["L0_ffn_W_out"],
        "b_out": a["L0_ffn_b_out"],
    }
    nc = bacc.Bacc("TRN2", target_bir_lowering=False, num_devices=1)
    aps = {n: nc.dram_tensor(n, v.shape, mybir.dt.from_np(v.dtype), kind="ExternalInput").ap()
           for n, v in laid_out.items()}
    out = nc.dram_tensor("out", _OUT, mybir.dt.float32, kind="ExternalOutput").ap()
    flamingo_layer(nc, out=out, **aps)
    r = run_bass_kernel_spmd(nc, [laid_out], core_ids=[0])
    return r.results[0]["out"]
```

```python
from contextlib import ExitStack

import concourse.bass as bass
from concourse import mybir


def flamingo_layer(nc, x, keys_dram, vals_dram, mask_cols, scalars, wo_t, w_gate, w_in, b_in,
                   w_out, b_out, out):
    f32 = mybir.dt.float32
    f32r = mybir.dt.float32r
    bf16 = mybir.dt.bfloat16
    i32 = mybir.dt.int32
    u32 = mybir.dt.uint32
    u8 = mybir.dt.uint8
    ALU = mybir.AluOpType
    ACT = mybir.ActivationFunctionType
    AX = mybir.AxisListType

    P = 128
    B, S, D = x.shape
    NK = vals_dram.shape[1]
    H = 16
    DH = D // H
    DC = D // P
    ST = S // P
    NT = B * ST
    TOK = B * S
    E = w_gate.shape[1]
    F = w_in.shape[2]
    FC = F // P
    TOPK = 2
    PARTS = ((0, 0), (0, 1), (1, 0))
    EPS = 1e-5
    MASKED = -1e30
    EXP_ROOM = 80.0

    ROWS = 32
    GH = 4
    NG = H // GH
    GW = GH * DH
    QH = P // ROWS

    SLOT = 256
    SS = SLOT // P
    MAXT = TOPK * TOK // SLOT + E
    PAY = D + 4
    NB = TOK // SLOT
    NPAIR = E // 2
    NC = 4
    CAP = TOK + SLOT
    LOADS = [(0, ST), (ST, 2 * ST), (2 * ST, NT // 2), (NT // 2, NT)]
    HP = FC // 2

    slots_dram = nc.dram_tensor("slot_rows", (E * CAP, PAY), f32, kind="Internal").ap()
    sums_dram = nc.dram_tensor("sum_rows", (TOK + SLOT, D), f32, kind="Internal").ap()

    with ExitStack() as stack:
        first_half = stack.enter_context(ExitStack())

        def sb(name, shape, dt=f32, until=stack):
            return until.enter_context(nc.sbuf_tensor(name, shape, dt))

        def sem(name):
            return stack.enter_context(nc.semaphore(name))

        def pair_of(make):
            return [make(0), make(1)]

        x_all = sb("x_all", [P, NT, D])
        ident = sb("ident", [P, P])
        scal = sb("scal", [P, 4])
        scal2 = sb("scal2", [P, 4])
        mask_u8 = sb("mask_u8", [NK, B], u8)
        key_bias = sb("key_bias", [NK, B])
        bias_now = pair_of(lambda i: sb(f"bias_now{i}", [NK, 1]))
        shift = sb("shift", [P, 1])
        wg_sb = sb("wg_sb", [P, DC, E])
        xn = sb("xn", [P, ST, D])
        bn1 = sb("bn1", [P, ST, 6])
        mv1 = sb("mv1", [P, ST, 2])
        ve1 = sb("ve1", [P, ST])
        rstd1 = sb("rstd1", [P, ST])
        bn2 = sb("bn2", [P, ST, 6])
        mv2 = sb("mv2", [P, ST, 2])
        ve2 = sb("ve2", [P, ST])
        rstd2 = sb("rstd2", [P, ST])
        minus_half = sb("minus_half", [P, ST])
        rsum = sb("rsum", [P, ST, H])
        pay = pair_of(lambda i: sb(f"pay{i}", [P, ST, PAY]))
        lg = sb("lg", [P, ST, E])
        top_v = sb("top_v", [P, ST, 8])
        top_i = sb("top_i", [P, ST, 8], u32)
        idx = sb("idx", [P, TOPK, ST])
        gap = sb("gap", [P, ST])
        egap = sb("egap", [P, ST])
        den = sb("den", [P, ST])
        onehot = sb("onehot", [P, TOPK, ST, E])
        member = sb("member", [P, ST, E], bf16)
        base = sb("base", [P, ST, E])
        pos = sb("pos", [P, ST, E])
        picked = sb("picked", [P, TOPK, ST, E])
        slot_f = sb("slot_f", [P, TOPK, ST])
        slot_i = pair_of(lambda i: sb(f"slot_i{i}", [P, TOPK, ST], i32))
        ones = sb("ones", [P, P])
        tri = sb("tri", [P, P], bf16)
        all_ones = sb("all_ones", [P, P], bf16)
        tok_id = sb("tok_id", [P, NT])
        e_iota = sb("e_iota", [P, TOPK * ST, E])
        first_row = sb("first_row", [P, E])
        t_iota = sb("t_iota", [P, E, NB])
        filled = sb("filled", [P, E])
        more = sb("more", [P, E, NB])
        n_tiles = sb("n_tiles", [P, E])
        n_scan = sb("n_scan", [P, E])
        start = sb("start", [P, E])
        plan = sb("plan", [1, 4 * E], i32)
        TOTAL = 2 * E - 1
        w_in_raw = pair_of(lambda i: sb(f"w_in_raw{i}", [P, DC, F]))
        w_out_raw = pair_of(lambda i: sb(f"w_out_raw{i}", [P, FC, D]))
        w_in_sb = [sb("w_in_sb0", [P, 2, DC, F], f32r)]
        w_out_sb = [sb("w_out_sb0", [P, 2, FC, D], f32r)]
        b_in_sb = sb("b_in_sb", [P, E, FC])
        b_in_now = pair_of(lambda i: sb(f"b_in_now{i}", [P, FC]))
        warm = sb("warm", [P, 1])
        b_out_sb = sb("b_out_sb", [P, E, D])
        pad = sb("pad", [P, SS, PAY])
        tail = sb("tail", [P, SS, PAY - D])
        second = sb("second", [P, SS])
        wdiff = sb("wdiff", [P, SS])
        wgt = sb("wgt", [P, SS])
        dest_f = sb("dest_f", [P, SS])
        dest_i = sb("dest_i", [P, SS], i32)
        probs = sb("probs", [NK, 2, H, S], until=first_half)
        keys_raw = pair_of(lambda i: sb(f"keys_raw{i}", [P, H, NK], until=first_half))
        keys = pair_of(lambda i: sb(f"keys{i}", [P, 2, H, NK], f32r, until=first_half))
        vals = pair_of(lambda i: sb(f"vals{i}", [NK, H, ROWS], until=first_half))
        mixed = sb("mixed", [P, QH, S], until=first_half)
        xq = sb("xq", [P, ST, NG, 2, GW], f32r, until=first_half)
        q_t = sb("q_t", [P, NG, S], f32r, until=first_half)
        att_t = sb("att_t", [P, DC, S], until=first_half)
        att = sb("att", [P, ST, D], until=first_half)
        xn2_t = sb("xn2_t", [P, DC, S], until=first_half)
        wo_sb = sb("wo_sb", [P, DC, D], until=first_half)
        first_half.close()
        w_in_sb.append(sb("w_in_sb1", [P, 2, DC, F], f32r))
        w_out_sb.append(sb("w_out_sb1", [P, 2, FC, D], f32r))
        xs = sb("xs", [P, SS, PAY])
        xs_t = sb("xs_t", [P, 2, DC, SLOT], f32r)
        hid = sb("hid", [P, FC, SLOT])
        hid_parts = sb("hid_parts", [P, 2, FC, SLOT], f32r)
        y_sb = sb("y_sb", [P, SS, D])

        bank = stack.enter_context(nc.psum_tensor("bank", [P, 8, 512], f32))
        SC = bank[:, 0:4, :]
        TQ = bank[:, 4, :]
        AT = bank[:, 5, :]
        AV = bank[:, 6:8, :]
        HB = [bank[:, i, :] for i in range(HP)]
        XT = bank[:, 4, :]
        YB = [bank[:, 6 + s, :] for s in range(SS)]

        def sems(*names):
            return [sem(n) for n in names]

        x_in = [sem(f"x_in{c}") for c in range(len(LOADS))]
        scal_in, mask_in, wo_in, wg_in, bias_in = sems("scal_in", "mask_in", "wo_in", "wg_in", "bias_in")
        keys_in = pair_of(lambda i: sem(f"keys_in{i}"))
        khi_done, klo_done, xf_done, xhi_done = sems("khi_done", "klo_done", "xf_done", "xhi_done")
        vals_in = pair_of(lambda i: sem(f"vals_in{i}"))
        ident_done, consts_done, pool_step, base_ready, pad_done = sems(
            "ident_done", "consts_done", "pool_step", "base_ready", "pad_done")
        scal_done, c_done, shift_done = sems("scal_done", "c_done", "shift_done")
        bn1_done, mv1_done, ve1_done, rstd1_done, xn_done, tq_done, qt_dve, qt_act, bias_now_done = sems(
            "bn1_done", "mv1_done", "ve1_done", "rstd1_done", "xn_done", "tq_done", "qt_dve", "qt_act",
            "bias_now_done")
        sc_done, tanh_done, exp_done, av_done, mixed_done, tu_done, rsum_done, att_done = sems(
            "sc_done", "tanh_done", "exp_done", "av_done", "mixed_done", "tu_done", "rsum_done", "att_done")
        ta_done, att_t_done, proj_done, x2_done, bn2_done, mv2_done, ve2_done, rstd2_done, xn2_done = sems(
            "ta_done", "att_t_done", "proj_done", "x2_done", "bn2_done", "mv2_done", "ve2_done", "rstd2_done",
            "xn2_done")
        t2_done, xn2_t_done, gate_done, lg_done, topv_done, topi_done, gap_done, egap_done = sems(
            "t2_done", "xn2_t_done", "gate_done", "lg_done", "topv_done", "topi_done", "gap_done", "egap_done")
        idx_done, w_done = sems("idx_done", "w_done")
        onehot_done, member_done, rank_done, base_done, rank_read, pos_done, picked_done, den_done = sems(
            "onehot_done", "member_done", "rank_done", "base_done", "rank_read", "pos_done", "picked_done",
            "den_done")
        slot_done, slots_done, route_step, plan_done, first_pad_out, pad_out, base_out = sems(
            "slot_done", "slots_done", "route_step", "plan_done", "first_pad_out", "pad_out", "base_out")
        sent = pair_of(lambda i: sem(f"sent{i}"))
        w_in_in = pair_of(lambda i: sem(f"w_in_in{i}"))
        w_out_in = pair_of(lambda i: sem(f"w_out_in{i}"))
        w_in_high, w_out_high, w_in_low, w_out_low, gelu_high, gelu_full, hid_low, xs_high = sems(
            "w_in_high", "w_out_high", "w_in_low", "w_out_low", "gelu_high", "gelu_full", "hid_low", "xs_high")
        b_in_done, xs_in, xs_free, tx_done, xs_t_done, h_done, y_done, y_sb_done = sems(
            "b_in_done", "xs_in", "xs_free", "tx_done", "xs_t_done", "h_done", "y_done", "y_sb_done")
        meta_step, yb_read, y_sent, y_free = sems("meta_step", "yb_read", "y_sent", "y_free")
        out_sent = sem("out_sent")

        x_view = x.rearrange("b (s p) d -> p (b s) d", p=P)
        out_rows = out.rearrange("b s d -> (b s) d")
        slots_view = slots_dram.rearrange("(e t s p) w -> e t p s w", e=E, s=SS, p=P)
        sums_view = sums_dram[0:TOK, :].rearrange("(t p) d -> p t d", p=P)
        w_in_view = w_in.rearrange("e (c p) f -> e p c f", p=P)
        w_out_view = w_out.rearrange("e (c p) d -> e p c d", p=P)
        def value(eng, v):
            return v if type(v) is int else eng.to_reg(v)

        def real(b):
            return type(b) is not int or 0 <= b < B

        def later(b, n):
            return type(b) is not int or b >= n

        def end_with_pad(eng, e, done):
            row = eng.value_load(plan[0:1, 2 * E + e:2 * E + e + 1], min_val=e * CAP, max_val=e * CAP + TOK)
            eng.dma_start(slots_dram[bass.ds(row, SLOT), :].rearrange("(s p) w -> p s w", p=P), pad[:, :, :]
                          ).then_inc(done, 16)

        def low_w_out_on(eng, e, i):
            eng.wait_ge(w_out_high, e + 1)
            eng.tensor_tensor(w_out_sb[i][:, 1, :, :], w_out_raw[i][:, :, :], w_out_sb[i][:, 0, :, :], ALU.subtract
                              ).then_inc(w_out_low, 1)

        def low_keys_on(eng, b, i):
            eng.wait_ge(khi_done, b + 1)
            eng.tensor_tensor(keys[i][:, 1, :, :], keys_raw[i][:, :, :], keys[i][:, 0, :, :], ALU.subtract
                              ).then_inc(klo_done, 1)

        block = stack.enter_context(nc.Block())

        @block.sync
        def _(sp):
            def load_x(c):
                t0, t1 = LOADS[c]
                sp.dma_start(x_all[:, t0:t1, :], x_view[:, t0:t1, :]).then_inc(x_in[c], 16)

            def load_keys(b, i):
                if later(b, 2):
                    sp.wait_ge(klo_done, b - 1)
                sp.dma_start(keys_raw[i][:, :, :], keys_dram[b]).then_inc(keys_in[i], 16)

            def load_vals(b, i):
                if later(b, 2):
                    sp.wait_ge(av_done, b - 1)
                sp.dma_start(vals[i][:, :, :], vals_dram[b]).then_inc(vals_in[i], 16)

            load_x(0)
            load_keys(0, 0)
            load_x(1)
            load_keys(1, 1)
            for c in range(2, len(LOADS)):
                load_x(c)
            load_vals(0, 0)
            load_vals(1, 1)
            with sp.Fori(0, (B - 2) // 2) as i:
                load_keys(2 * i + 2, 0)
                load_vals(2 * i + 2, 0)
                load_keys(2 * i + 3, 1)
                load_vals(2 * i + 3, 1)
            with sp.Fori(0, B) as b:
                sp.wait_ge(x2_done, b + 1)
                sp.dma_start(sums_view[:, bass.ds(b * ST, ST), :], x_all[:, bass.ds(b * ST, ST), :]).then_inc(base_out, 16)
            sp.wait_ge(pad_done, 2 + SS)
            sp.dma_start(sums_dram[TOK:TOK + SLOT, :].rearrange("(s p) d -> p s d", p=P), pad[:, :, 0:D]
                         ).then_inc(base_out, 16)
            sp.wait_ge(plan_done, 1)
            end_with_pad(sp, 0, first_pad_out)
            sp.wait_ge(first_pad_out, 16)
            for i in range(2):
                sp.wait_ge(sent[i], 16 * TOPK * NT // 2)

            def load_slots(e):
                first = sp.value_load(plan[0:1, bass.ds(e, 1)], min_val=0, max_val=MAXT)
                count = sp.value_load(plan[0:1, bass.ds(e + 3 * E, 1)], min_val=1, max_val=NB)
                with sp.Fori(0, count) as t:
                    sp.wait_ge(xs_free, first + t + 1)
                    sp.dma_start(xs[:, :, :], slots_view[e, t]).then_inc(xs_in, 16)

            def next_weights(e, i):
                sp.wait_ge(w_in_low, e + 1)
                sp.dma_start(w_in_raw[i][:, :, :], w_in_view[e + 2]).then_inc(w_in_in[i], 16)
                sp.wait_ge(w_out_low, e + 1)
                sp.dma_start(w_out_raw[i][:, :, :], w_out_view[e + 2]).then_inc(w_out_in[i], 16)

            load_slots(0)
            next_weights(0, 0)
            sp.wait_ge(pad_out, 16 * (E - 1))
            load_slots(1)
            next_weights(1, 1)
            with sp.Fori(1, NPAIR - 1) as i:
                load_slots(2 * i)
                next_weights(2 * i, 0)
                load_slots(2 * i + 1)
                next_weights(2 * i + 1, 1)
            load_slots(E - 2)
            load_slots(E - 1)
            total = sp.value_load(plan[0:1, TOTAL:TOTAL + 1], min_val=E, max_val=MAXT)
            sp.wait_ge(xs_free, total + 1)
            sp.dma_start(xs[:, :, :], slots_view[0, 0]).then_inc(xs_in, 16)
            sp.wait_ge(y_sent, total * (16 * SS))
            for c in range(NC):
                rows = slice(c * TOK // NC, (c + 1) * TOK // NC)
                sp.dma_start(out_rows[rows, :], sums_dram[rows, :]).then_inc(out_sent, 16)
            sp.wait_ge(out_sent, 16 * NC)

        @block.gpsimd
        def _(pool):
            pool.memset(minus_half[:, :], -0.5).then_inc(pool_step, 1)
            pool.memset(ident[:, :], 0.0).then_inc(pool_step, 1)
            pool.wait_ge(pool_step, 2)
            pool.affine_select(out=ident[:, :], in_=ident[:, :], compare_op=ALU.not_equal, fill=1.0, base=0,
                               pattern=[[-1, P]], channel_multiplier=1).then_inc(ident_done, 1)

            def rstd(b, mv, ve, done_in, ve_done, r, done_out):
                after = value(pool, b + 1)
                pool.wait_ge(ident_done, 1)
                pool.wait_ge(done_in, after)
                pool.tensor_scalar(ve[:, :], mv[:, :, 1], EPS, None, ALU.add).then_inc(ve_done, 1)
                pool.wait_ge(ve_done, b + 1)
                pool.tensor_tensor(r[:, :], ve[:, :], minus_half[:, :], ALU.pow).then_inc(done_out, 1)

            def step(b, i):
                if real(b + 1):
                    low_keys_on(pool, b + 1, 1 - i)
                if real(b - 2):
                    rstd(b - 2, mv2, ve2, mv2_done, ve2_done, rstd2, rstd2_done)
                if real(b + 2):
                    rstd(b + 2, mv1, ve1, mv1_done, ve1_done, rstd1, rstd1_done)
                if real(b - 3):
                    send(b - 3, 1 - i)

            def send(b, i):
                after = value(pool, b + 1)
                pool.wait_ge(ident_done, 1)
                pool.wait_ge(slots_done, after)
                for k in range(TOPK):
                    for s in range(ST):
                        pool.indirect_dma_start(
                            out=slots_dram,
                            out_offset=bass.IndirectOffsetOnAxis(ap=slot_i[i][:, k, s:s + 1], axis=0),
                            in_=pay[i][:, s, :], in_offset=None).then_inc(sent[i], 16)

            rstd(0, mv1, ve1, mv1_done, ve1_done, rstd1, rstd1_done)
            rstd(1, mv1, ve1, mv1_done, ve1_done, rstd1, rstd1_done)
            step(0, 0)
            pool.memset(ones[:, :], 1.0).then_inc(pool_step, 1)
            pool.wait_ge(pool_step, 3)
            pool.tensor_copy(all_ones[:, :], ones[:, :])
            pool.affine_select(out=tri[:, :], in_=ones[:, :], compare_op=ALU.is_gt, fill=0.0, base=0,
                               pattern=[[1, P]], channel_multiplier=-1)
            iota = dict(base=0, allow_small_or_imprecise_dtypes=True)
            pool.iota(base[:, 0, :], [[CAP, E]], channel_multiplier=0, **iota)
            pool.iota(first_row[:, :], [[CAP, E]], channel_multiplier=0, **iota)
            pool.iota(tok_id[:, :], [[P, NT]], channel_multiplier=1, **iota)
            pool.iota(e_iota[:, :, :], [[0, TOPK * ST], [1, E]], channel_multiplier=0, **iota)
            pool.iota(t_iota[:, :, :], [[0, E], [SLOT, NB]], channel_multiplier=0, **iota
                      ).then_inc(consts_done, 1)
            step(1, 1)
            pool.memset(pad[:, :, 0:D + 2], 0.0).then_inc(pad_done, 1)
            pool.memset(pad[:, :, D + 2:D + 3], -1.0).then_inc(pad_done, 1)
            for s in range(SS):
                pool.iota(pad[:, s, D + 3:D + 4], [[0, 1]], base=TOK + s * P, channel_multiplier=1,
                          allow_small_or_imprecise_dtypes=True).then_inc(pad_done, 1)
            step(2, 0)
            step(3, 1)
            with pool.Fori(0, (B - 6) // 2) as i:
                step(2 * i + 4, 0)
                step(2 * i + 5, 1)
            for b in range(B - 2, B + 3):
                step(b, b % 2)
            pool.wait_ge(plan_done, 1)
            pool.wait_ge(base_out, 16 * (B + 1))
            pool.nop().then_inc(y_free, 1)
            def results(t):
                after = value(pool, t + 1)
                pool.wait_ge(plan_done, 1)
                pool.wait_ge(y_sb_done, after)
                for s in range(SS):
                    pool.indirect_dma_start(
                        out=sums_dram, out_offset=bass.IndirectOffsetOnAxis(ap=dest_i[:, s:s + 1], axis=0),
                        in_=y_sb[:, s, :], in_offset=None, compute_op=ALU.add).then_inc(y_sent, 16)
                pool.wait_ge(y_sent, t * (16 * SS) + 16 * SS)
                pool.nop().then_inc(y_free, 1)

            def expert(e, i, more=True):
                if more:
                    low_w_out_on(pool, e + 1, 1 - i)
                first = pool.value_load(plan[0:1, bass.ds(e, 1)], min_val=0, max_val=MAXT)
                end = pool.value_load(plan[0:1, bass.ds(e + E, 1)], min_val=1, max_val=MAXT)
                with pool.Fori(first, end) as t:
                    results(t)

            with pool.Fori(0, NPAIR - 1) as i:
                expert(2 * i, 0)
                expert(2 * i + 1, 1)
            expert(E - 2, 0)
            expert(E - 1, 1, more=False)

        @block.scalar
        def _(act):
            act.dma_start(scal[:, :], scalars.partition_broadcast(P)).then_inc(scal_in, 16)
            act.dma_start(mask_u8[:, :], mask_cols).then_inc(mask_in, 16)
            act.wait_ge(scal_in, 16)
            act.activation(scal2[:, 2:4], scal[:, 2:4], ACT.Tanh).then_inc(scal_done, 1)
            act.activation(scal2[:, 0:1], scal[:, 0:1], ACT.Copy, scale=float(DH) ** -0.5
                           ).then_inc(scal_done, 1)
            act.activation(scal2[:, 1:2], scal[:, 1:2], ACT.Exp).then_inc(c_done, 1)
            act.wait_ge(scal_done, 2)
            act.wait_ge(c_done, 1)

            def queries(b):
                act.wait_ge(tq_done, b + 1)
                if later(b, 1):
                    act.wait_ge(sc_done, b * NG)
                act.activation(q_t[:, 2:4, :], SC[:, 1, :].rearrange("p (j q) -> p j q", q=S), ACT.Copy
                               ).then_inc(qt_act, 1)

            def bounded(b, i, g):
                if g == 0 and later(b, 2):
                    act.wait_ge(av_done, b - 1)
                act.wait_ge(sc_done, b * NG + (g + 1))
                act.activation(probs[:, i, g * GH:(g + 1) * GH, :],
                               SC[0:NK, 2 * (g % 2):2 * (g % 2) + 2, :].rearrange("k r (h q) -> k (r h) q", q=S),
                               ACT.Tanh, scale=scal2[0:NK, 0:1]).then_inc(tanh_done, 1)

            def weigh(b, i, half):
                act.wait_ge(bias_now_done, b + 1)
                act.wait_ge(tanh_done, b * NG + (2 * half + 2))
                both = probs[:, i, 2 * half * GH:(2 * half + 2) * GH, :]
                act.activation(both, both, ACT.Exp, bias=bias_now[i][:, :], scale=scal2[0:NK, 1:2]
                               ).then_inc(exp_done, 1)

            def choice(b):
                act.wait_ge(gap_done, b + 1)
                act.activation(egap[:, :], gap[:, :], ACT.Exp).then_inc(egap_done, 1)

            def xn2_turned(b):
                act.wait_ge(t2_done, b + 1)
                act.activation(xn2_t[:, :, :], TQ.rearrange("p (c q) -> p c q", c=DC), ACT.Copy
                               ).then_inc(xn2_t_done, 1)

            def step(b, i):
                if real(b):
                    bounded(b, i, 0)
                    bounded(b, i, 1)
                    weigh(b, i, 0)
                if real(b - 3):
                    choice(b - 3)
                if real(b):
                    bounded(b, i, 2)
                    bounded(b, i, 3)
                if real(b + 1):
                    queries(b + 1)
                if real(b):
                    weigh(b, i, 1)
                if real(b - 2):
                    xn2_turned(b - 2)

            act.wait_ge(keys_in[0], 16)
            act.activation(keys[0][:, 0, :, :], keys_raw[0][:, :, :], ACT.Copy).then_inc(khi_done, 1)
            queries(0)
            step(0, 0)
            act.dma_start(wo_sb[:, :, :], wo_t.rearrange("(c p) f -> p c f", p=P)).then_inc(wo_in, 16)
            act.dma_start(wg_sb[:, :, :], w_gate.rearrange("(c p) e -> p c e", p=P)).then_inc(wg_in, 16)
            step(1, 1)
            act.dma_start(b_in_sb[:, :, :], b_in).then_inc(bias_in, 16)
            act.dma_start(w_in_raw[0][:, :, :], w_in_view[0]).then_inc(w_in_in[0], 16)
            step(2, 0)
            act.dma_start(w_out_raw[0][:, :, :], w_out_view[0]).then_inc(w_out_in[0], 16)
            step(3, 1)
            act.dma_start(b_out_sb[:, :, :], b_out.partition_broadcast(P)).then_inc(bias_in, 16)
            with act.Fori(0, (B - 6) // 2) as i:
                step(2 * i + 4, 0)
                step(2 * i + 5, 1)
            act.dma_start(w_in_raw[1][:, :, :], w_in_view[1]).then_inc(w_in_in[1], 16)
            act.dma_start(w_out_raw[1][:, :, :], w_out_view[1]).then_inc(w_out_in[1], 16)
            for b in range(B - 2, B + 3):
                step(b, b % 2)

            def expert(e, i):
                first = act.value_load(plan[0:1, bass.ds(e, 1)], min_val=0, max_val=MAXT)
                end = act.value_load(plan[0:1, bass.ds(e + E, 1)], min_val=1, max_val=MAXT)
                act.wait_ge(b_in_done, e + 1)
                with act.Fori(first, end) as t:
                    for m in range(0, FC, 2):
                        act.wait_ge(h_done, t * HP + (m // 2 + 1))
                        for out, done in ((hid_parts[:, 0], gelu_high), (hid, gelu_full)):
                            for k in range(2):
                                ins = act.activation(out[:, m + k, :], HB[m // 2][:, k * SLOT:(k + 1) * SLOT],
                                                     ACT.Gelu, bias=b_in_now[i][:, m + k:m + k + 1])
                            ins.then_inc(done, 1)

            act.wait_ge(pad_done, 2 + SS)
            act.wait_ge(plan_done, 1)
            for e in range(1, E):
                end_with_pad(act, e, pad_out)
            act.activation(warm[:, :], scal2[:, 0:1], ACT.Gelu)
            with act.Fori(0, NPAIR) as i:
                expert(2 * i, 0)
                expert(2 * i + 1, 1)
        @block.vector
        def _(dve):
            def rows(b, s):
                return x_all[:, bass.ds(b * ST + s, 1), :].squeeze(1)

            def stats(b, bn, mv, bnd, mvd):
                after = value(dve, b + 1)
                dve.wait_ge(x_in[0], 16)
                if bnd is bn2_done:
                    dve.wait_ge(x2_done, after)
                for s in range(ST):
                    ins = dve.bn_stats(bn[:, s, :], rows(b, s))
                ins.then_inc(bnd, 1)
                dve.wait_ge(x_in[0], 16)
                dve.wait_ge(bnd, after)
                for s in range(ST):
                    ins = dve.bn_aggr(mv[:, s, :], bn[:, s, :])
                ins.then_inc(mvd, 1)

            def stats1(b):
                stats(b, bn1, mv1, bn1_done, mv1_done)

            def norm1(b):
                dve.wait_ge(rstd1_done, b + 1)
                if later(b, 1):
                    dve.wait_ge(xn_done, b)
                    dve.wait_ge(tq_done, b)
                for s in range(ST):
                    ins = dve.tensor_scalar(xn[:, s, :], rows(b, s), mv1[:, s, 0:1], rstd1[:, s:s + 1],
                                            ALU.subtract, ALU.mult)
                ins.then_inc(xf_done, 1)
                full = xn[:, :, :].rearrange("p s (g w) -> p (s g) w", w=GW)
                parts = xq[:, :, :, :, :].rearrange("p s g t w -> p (s g) t w")
                dve.wait_ge(xf_done, b + 1)
                dve.tensor_copy(parts[:, :, 0, :], full).then_inc(xhi_done, 1)
                dve.wait_ge(xhi_done, b + 1)
                dve.tensor_tensor(parts[:, :, 1, :], full, parts[:, :, 0, :], ALU.subtract).then_inc(xn_done, 1)

            def high_keys(b, i, n):
                if later(b, 2):
                    dve.wait_ge(sc_done, (b - 1) * NG)
                dve.wait_ge(keys_in[i], 16 * n + 16)
                dve.tensor_copy(keys[i][:, 0, :, :], keys_raw[i][:, :, :]).then_inc(khi_done, 1)

            def query(b):
                dve.wait_ge(tq_done, b + 1)
                if later(b, 1):
                    dve.wait_ge(sc_done, b * NG)
                dve.tensor_copy(q_t[:, 0:2, :], SC[:, 0, :].rearrange("p (j q) -> p j q", q=S)).then_inc(qt_dve, 1)

            def key_bias_now(b, i):
                if later(b, 2):
                    dve.wait_ge(exp_done, 2 * b - 2)
                dve.tensor_copy(bias_now[i][:, :], key_bias[:, bass.ds(b, 1)]).then_inc(bias_now_done, 1)

            def mixed_out(b):
                dve.wait_ge(av_done, b + 1)
                dve.tensor_copy(mixed[:, :, :].rearrange("p (s g) q -> p s (g q)", s=ST), AV).then_inc(mixed_done, 1)

            def attend(b):
                dve.wait_ge(tu_done, b + 1)
                turned_v = AV.rearrange("p s (h w) -> p s h w", w=ROWS)
                dve.reciprocal(rsum[:, :, :], turned_v[:, :, :, DH]).then_inc(rsum_done, 1)
                dve.wait_ge(rsum_done, b + 1)
                for s in range(ST):
                    ins = dve.tensor_tensor(att[:, s, :].rearrange("p (h d) -> p h d", h=H),
                                            turned_v[:, s, :, 0:DH],
                                            rsum[:, s, :].unsqueeze(2).to_broadcast([P, H, DH]), ALU.mult)
                ins.then_inc(att_done, 1)

            def att_turned(b):
                dve.wait_ge(ta_done, b + 1)
                dve.tensor_copy(att_t[:, :, :], AT.rearrange("p (c q) -> p c q", c=DC)).then_inc(att_t_done, 1)

            def residual(b):
                dve.wait_ge(proj_done, b + 1)
                for s in range(ST):
                    ins = dve.scalar_tensor_tensor(rows(b, s), AT[:, s * D:(s + 1) * D], scal2[:, 2:3], rows(b, s),
                                                   ALU.mult, ALU.add)
                ins.then_inc(x2_done, 1)
                stats(b, bn2, mv2, bn2_done, mv2_done)

            def norm2(b, i, n):
                if later(b, 2):
                    dve.wait_ge(sent[i], n * (16 * TOPK * ST))
                dve.wait_ge(rstd2_done, b + 1)
                for s in range(ST):
                    ins = dve.tensor_scalar(pay[i][:, s, 0:D], rows(b, s), mv2[:, s, 0:1], rstd2[:, s:s + 1],
                                            ALU.subtract, ALU.mult)
                ins.then_inc(xn2_done, 1)

            def choose(b):
                dve.wait_ge(gate_done, b + 1)
                dve.tensor_copy(lg[:, :, :], TQ[:, 0:ST * E].rearrange("p (s e) -> p s e", s=ST)).then_inc(lg_done, 1)
                after = value(dve, b + 1)
                dve.wait_ge(x_in[0], 16)
                dve.wait_ge(lg_done, after)
                for s in range(ST):
                    ins = dve.max(top_v[:, s, :], lg[:, s, :])
                ins.then_inc(topv_done, 1)
                dve.wait_ge(x_in[0], 16)
                dve.wait_ge(topv_done, after)
                for s in range(ST):
                    ins = dve.max_index(top_i[:, s, :], top_v[:, s, :], lg[:, s, :])
                ins.then_inc(topi_done, 1)
                dve.tensor_tensor(gap[:, :], top_v[:, :, 1], top_v[:, :, 0], ALU.subtract).then_inc(gap_done, 1)
                dve.wait_ge(topi_done, after)
                dve.tensor_copy(idx[:, :, :].rearrange("p k s -> p s k"), top_i[:, :, 0:TOPK]).then_inc(idx_done, 1)
                dve.wait_ge(idx_done, after)
                dve.tensor_tensor(onehot[:, :, :, :].rearrange("p k s e -> p (k s) e"),
                                  idx[:, :, :].rearrange("p k s -> p (k s)").unsqueeze(2).to_broadcast([P, TOPK * ST, E]),
                                  e_iota[:, :, :], ALU.is_equal).then_inc(onehot_done, 1)
                dve.wait_ge(onehot_done, after)
                dve.tensor_tensor(member[:, :, :], onehot[:, 0, :, :], onehot[:, 1, :, :], ALU.add
                                  ).then_inc(member_done, 1)

            def slots(b, i):
                dve.wait_ge(egap_done, b + 1)
                dve.tensor_scalar(den[:, :], egap[:, :], 1.0, None, ALU.add).then_inc(den_done, 1)
                after = value(dve, b + 1)
                dve.wait_ge(rank_done, after)
                in_tile = TQ[:, 0:ST * E].rearrange("p (s e) -> p s e", s=ST)
                of_tile = TQ[:, ST * E:2 * ST * E].rearrange("p (s e) -> p s e", s=ST)
                dve.tensor_tensor(base[:, 1, :], base[:, 0, :], of_tile[:, 0, :], ALU.add).then_inc(base_done, 1)
                dve.wait_ge(den_done, 2 * b + 1)
                dve.reciprocal(den[:, :], den[:, :]).then_inc(den_done, 1)
                dve.wait_ge(base_done, b + 1)
                dve.tensor_tensor(pos[:, :, :], in_tile, base[:, :, :], ALU.add).then_inc(pos_done, 1)
                dve.wait_ge(den_done, 2 * b + 2)
                dve.tensor_scalar(pay[i][:, :, D], den[:, :], scal2[:, 3:4], None, ALU.mult).then_inc(w_done, 1)
                dve.wait_ge(pos_done, after)
                dve.tensor_tensor(base[:, 0, :], base[:, 1, :], of_tile[:, 1, :], ALU.add).then_inc(rank_read, 1)
                dve.tensor_tensor(picked[:, :, :, :].rearrange("p k s e -> p k (s e)"),
                                  onehot[:, :, :, :].rearrange("p k s e -> p k (s e)"),
                                  pos[:, :, :].rearrange("p s e -> p (s e)").unsqueeze(1).to_broadcast([P, TOPK, ST * E]),
                                  ALU.mult).then_inc(picked_done, 1)
                dve.wait_ge(w_done, after)
                dve.tensor_tensor(pay[i][:, :, D + 1], pay[i][:, :, D], egap[:, :], ALU.mult)
                dve.wait_ge(picked_done, after)
                dve.tensor_reduce(slot_f[:, :, :].rearrange("p k s -> p (k s)"),
                                  picked[:, :, :, :].rearrange("p k s e -> p (k s) e"), axis=AX.X, op=ALU.add
                                  ).then_inc(slot_done, 1)
                dve.tensor_copy(pay[i][:, :, D + 2], idx[:, 0, :])
                dve.tensor_copy(pay[i][:, :, D + 3], tok_id[:, bass.ds(b * ST, ST)])
                dve.wait_ge(slot_done, after)
                dve.tensor_copy(slot_i[i][:, :, :], slot_f[:, :, :]).then_inc(slots_done, 1)

            def b_in_of(e, i):
                dve.tensor_copy(b_in_now[i][:, :], b_in_sb[:, bass.ds(e, 1), :].squeeze(1)).then_inc(b_in_done, 1)

            def split_weights(e, i, n):
                dve.wait_ge(w_out_in[i], n * 16 + 16)
                dve.tensor_copy(w_out_sb[i][:, 0, :, :], w_out_raw[i][:, :, :]).then_inc(w_out_high, 1)
                dve.wait_ge(w_in_in[i], n * 16 + 16)
                dve.tensor_copy(w_in_sb[i][:, 0, :, :], w_in_raw[i][:, :, :]).then_inc(w_in_high, 1)
                dve.wait_ge(w_in_high, e + 1)
                dve.tensor_tensor(w_in_sb[i][:, 1, :, :], w_in_raw[i][:, :, :], w_in_sb[i][:, 0, :, :],
                                  ALU.subtract).then_inc(w_in_low, 1)

            dve.wait_ge(x_in[0], 16)
            stats1(0)
            norm1(0)
            low_keys_on(dve, 0, 0)
            query(0)
            dve.wait_ge(c_done, 1)
            dve.tensor_scalar(shift[:, :], scal2[:, 1:2], -1.0, EXP_ROOM, ALU.mult, ALU.add
                              ).then_inc(shift_done, 1)
            dve.wait_ge(shift_done, 1)
            dve.tensor_scalar(shift[:, :], shift[:, :], 0.0, None, ALU.min).then_inc(shift_done, 1)
            dve.wait_ge(shift_done, 2)
            dve.wait_ge(mask_in, 16)
            dve.tensor_scalar(key_bias[:, :], mask_u8[:, :], MASKED, shift[0:NK, :], ALU.mult, ALU.add
                              ).then_inc(shift_done, 1)
            dve.wait_ge(shift_done, 3)
            dve.memset(tail[:, :, :], 0.0).then_inc(xs_free, 1)
            dve.memset(wgt[:, :], 0.0).then_inc(yb_read, 1)

            def step(b, i, n):
                if real(b):
                    key_bias_now(b, i)
                if real(b + 1):
                    high_keys(b + 1, 1 - i, n + 1 if i else n)
                    norm1(b + 1)
                if real(b - 3):
                    choose(b - 3)
                if real(b - 2):
                    residual(b - 2)
                if real(b - 1):
                    mixed_out(b - 1)
                if real(b - 2):
                    norm2(b - 2, i, n - 1)
                if real(b - 3):
                    slots(b - 3, 1 - i)
                if real(b + 2):
                    stats1(b + 2)
                if real(b - 1):
                    attend(b - 1)
                if real(b + 1):
                    query(b + 1)
                if real(b - 1):
                    att_turned(b - 1)

            dve.wait_ge(x_in[1], 16)
            stats1(1)
            dve.wait_ge(x_in[2], 16)
            step(0, 0, 0)
            dve.wait_ge(x_in[3], 16)
            step(1, 1, 0)
            dve.wait_ge(scal_done, 2)
            step(2, 0, 1)
            dve.wait_ge(consts_done, 1)
            step(3, 1, 1)
            with dve.Fori(0, (B - 6) // 2) as i:
                step(2 * i + 4, 0, i + 2)
                step(2 * i + 5, 1, i + 2)
            step(B - 2, 0, B // 2 - 1)
            step(B - 1, 1, B // 2 - 1)
            step(B, 0, B // 2)
            step(B + 1, 1, B // 2)
            step(B + 2, 0, B // 2 + 1)

            count = [0]

            def link(ins):
                count[0] += 1
                ins.then_inc(route_step, 1)
                dve.wait_ge(route_step, count[0])

            dve.wait_ge(rank_read, B)
            link(dve.tensor_tensor(filled[:, :], base[:, 0, :], first_row[:, :], ALU.subtract))
            link(dve.tensor_tensor(more[:, :, :], filled[:, :].unsqueeze(2).to_broadcast([P, E, NB]),
                                   t_iota[:, :, :], ALU.is_gt))
            link(dve.tensor_reduce(n_tiles[:, :], more[:, :, :], axis=AX.X, op=ALU.add))
            link(dve.tensor_scalar(n_tiles[:, :], n_tiles[:, :], 1.0, None, ALU.max))
            link(dve.tensor_tensor_scan(n_scan[:, :], ones[:, 0:E], n_tiles[:, :], 0.0, ALU.mult, ALU.add))
            link(dve.tensor_tensor(start[:, :], n_scan[:, :], n_tiles[:, :], ALU.subtract))
            dve.tensor_copy(plan[0:1, 0:E], start[0:1, :])
            dve.tensor_copy(plan[0:1, E:2 * E], n_scan[0:1, :])
            dve.tensor_copy(plan[0:1, 2 * E:3 * E], base[0:1, 0, :])
            dve.tensor_copy(plan[0:1, 3 * E:4 * E], n_tiles[0:1, :]).then_inc(plan_done, 1)
            split_weights(0, 0, 0)
            low_w_out_on(dve, 0, 0)

            def turned(t):
                dve.wait_ge(tx_done, t + 1)
                turned_x = XT.rearrange("p (c q) -> p c q", c=DC)
                dve.tensor_copy(xs_t[:, 0, :, :], turned_x).then_inc(xs_high, 1)
                dve.wait_ge(xs_high, t + 1)
                dve.tensor_tensor(xs_t[:, 1, :, :], turned_x, xs_t[:, 0, :, :], ALU.subtract).then_inc(xs_t_done, 1)

            def keep_tail(t):
                if later(t, 1):
                    dve.wait_ge(meta_step, 5 * t)
                dve.tensor_copy(tail[:, :, :], xs[:, :, D:PAY]).then_inc(xs_free, 1)

            def meta(e, t):
                dve.wait_ge(xs_free, t + 2)
                dve.tensor_scalar(second[:, :], tail[:, :, 2], e_iota[:, 0, bass.ds(e, 1)], None, ALU.not_equal
                                  ).then_inc(meta_step, 1)
                dve.tensor_tensor(wdiff[:, :], tail[:, :, 1], tail[:, :, 0], ALU.subtract).then_inc(meta_step, 1)
                dve.wait_ge(meta_step, 5 * t + 2)
                dve.tensor_tensor(wdiff[:, :], wdiff[:, :], second[:, :], ALU.mult).then_inc(meta_step, 1)
                dve.tensor_copy(dest_f[:, :], tail[:, :, 3]).then_inc(meta_step, 1)
                dve.wait_ge(meta_step, 5 * t + 4)
                dve.tensor_tensor(wgt[:, :], wdiff[:, :], tail[:, :, 0], ALU.add).then_inc(meta_step, 1)

            def expert(e, i, n, more=True):
                first = dve.value_load(plan[0:1, bass.ds(e, 1)], min_val=0, max_val=MAXT)
                end = dve.value_load(plan[0:1, bass.ds(e + E, 1)], min_val=1, max_val=MAXT)
                if more:
                    b_in_of(e + 1, 1 - i)
                    split_weights(e + 1, 1 - i, n + 1 if i else n)
                with dve.Fori(first, end) as t:
                    for m in range(HP):
                        dve.wait_ge(gelu_full, t * HP + (m + 1))
                        dve.tensor_tensor(hid_parts[:, 1, 2 * m:2 * m + 2, :], hid[:, 2 * m:2 * m + 2, :],
                                          hid_parts[:, 0, 2 * m:2 * m + 2, :], ALU.subtract).then_inc(hid_low, 1)
                    turned(t + 1)
                    meta(e, t)
                    keep_tail(t + 1)
                    dve.wait_ge(y_done, t + 1)
                    dve.wait_ge(y_free, t + 1)
                    for s in range(SS):
                        ins = dve.tensor_tensor(y_sb[:, s, :], YB[s][:, 0:D], b_out_sb[:, bass.ds(e, 1), :].squeeze(1),
                                                ALU.add)
                    ins.then_inc(yb_read, 1)
                    dve.tensor_copy(dest_i[:, :], dest_f[:, :])
                    dve.wait_ge(yb_read, t + 2)
                    for s in range(SS):
                        ins = dve.tensor_scalar(y_sb[:, s, :], y_sb[:, s, :], wgt[:, s:s + 1], None, ALU.mult)
                    ins.then_inc(y_sb_done, 1)

            dve.wait_ge(bias_in, 32)
            b_in_of(0, 0)
            turned(0)
            keep_tail(0)
            with dve.Fori(0, NPAIR - 1) as i:
                expert(2 * i, 0, i)
                expert(2 * i + 1, 1, i)
            expert(E - 2, 0, NPAIR - 1)
            expert(E - 1, 1, NPAIR - 1, more=False)

        @block.tensor
        def _(pe):
            def turn(dst, src):
                for s in range(ST):
                    for c in range(DC):
                        ins = pe.transpose(dst[:, c * S + s * P:c * S + (s + 1) * P], src[:, s, c * P:(c + 1) * P],
                                           ident[:, :])
                return ins

            def turn_queries(b):
                pe.wait_ge(xn_done, b + 1)
                if later(b, 1):
                    pe.wait_ge(tanh_done, b * NG - 1)
                for g in range(NG):
                    for s in range(ST):
                        q0 = (g % 2) * S + s * P
                        ins = pe.transpose(SC[:, g // 2, q0:q0 + P],
                                           xq[:, s, g, :, :].rearrange("p t w -> p (t w)").bitcast(f32), ident[:, :])
                ins.then_inc(tq_done, 1)

            def scores(b, i, g):
                if g == 0:
                    pe.wait_ge(klo_done, b + 1)
                    pe.wait_ge(qt_dve, b + 1)
                    pe.wait_ge(qt_act, b + 1)
                else:
                    if later(b, 1) or g >= 2:
                        pe.wait_ge(tanh_done, b * NG + (g - 1))
                for h in range(GH):
                    for part in range(2):
                        ins = pe.matmul(SC[0:NK, 2 * (g % 2) + h // 2, (h % 2) * S:(h % 2 + 1) * S],
                                        keys[i][:, part, g * GH + h, :], q_t[:, g, :],
                                        start=(part == 0), stop=(part == 1))
                ins.then_inc(sc_done, 1)

            def values(b, i, half, n):
                pe.wait_ge(exp_done, 2 * b + (half + 1))
                if half == 0:
                    pe.wait_ge(vals_in[i], (n + 1) * 16)
                    if later(b, 1):
                        pe.wait_ge(att_done, b)
                for h in range(half * H // 2, (half + 1) * H // 2):
                    g, j = h // QH, h % QH
                    ins = pe.matmul(AV[j * ROWS:(j + 1) * ROWS, g // 2, (g % 2) * S:(g % 2 + 1) * S],
                                    vals[i][:, h, :], probs[:, i, h, :], start=True, stop=True)
                if half:
                    ins.then_inc(av_done, 1)

            def turn_mixed(b):
                pe.wait_ge(mixed_done, b + 1)
                for s in range(ST):
                    for g in range(QH):
                        ins = pe.transpose(AV[:, s, g * P:(g + 1) * P], mixed[:, g, s * P:(s + 1) * P], ident[:, :])
                ins.then_inc(tu_done, 1)

            def turn_att(b):
                pe.wait_ge(att_done, b + 1)
                if later(b, 1):
                    pe.wait_ge(x2_done, b)
                turn(AT, att).then_inc(ta_done, 1)

            def project(b):
                pe.wait_ge(att_t_done, b + 1)
                for s in range(ST):
                    for c in range(DC):
                        ins = pe.matmul(AT[:, s * D:(s + 1) * D], att_t[:, c, s * P:(s + 1) * P], wo_sb[:, c, :],
                                        start=(c == 0), stop=(c == DC - 1))
                ins.then_inc(proj_done, 1)

            def turn_xn2(b, i):
                pe.wait_ge(xn2_done, b + 1)
                if later(b, 1):
                    pe.wait_ge(rank_read, b)
                turn(TQ, pay[i]).then_inc(t2_done, 1)

            def gate(b):
                pe.wait_ge(xn2_t_done, b + 1)
                for s in range(ST):
                    for c in range(DC):
                        ins = pe.matmul(TQ[:, s * E:(s + 1) * E], xn2_t[:, c, s * P:(s + 1) * P], wg_sb[:, c, :],
                                        start=(c == 0), stop=(c == DC - 1))
                ins.then_inc(gate_done, 1)

            def rank(b):
                pe.wait_ge(member_done, b + 1)
                flat = member[:, :, :].rearrange("p s e -> p (s e)")
                pe.matmul(TQ[:, 0:ST * E], tri[:, :], flat, start=True, stop=True)
                pe.matmul(TQ[:, ST * E:2 * ST * E], all_ones[:, :], flat, start=True, stop=True).then_inc(rank_done, 1)

            def step(b, i, n):
                if real(b):
                    scores(b, i, 0)
                    scores(b, i, 1)
                if real(b - 3):
                    gate(b - 3)
                if real(b - 2):
                    project(b - 2)
                if real(b - 1):
                    values(b - 1, 1 - i, 0, n if i else n - 1)
                    values(b - 1, 1 - i, 1, n if i else n - 1)
                if real(b):
                    scores(b, i, 2)
                    scores(b, i, 3)
                if real(b - 3):
                    rank(b - 3)
                if real(b - 1):
                    turn_mixed(b - 1)
                if real(b + 1):
                    turn_queries(b + 1)
                if real(b - 2):
                    turn_xn2(b - 2, i)
                if real(b - 1):
                    turn_att(b - 1)

            pe.wait_ge(ident_done, 1)
            turn_queries(0)
            step(0, 0, 0)
            step(1, 1, 0)
            pe.wait_ge(wo_in, 16)
            step(2, 0, 1)
            pe.wait_ge(wg_in, 16)
            pe.wait_ge(consts_done, 1)
            step(3, 1, 1)
            with pe.Fori(0, (B - 6) // 2) as i:
                step(2 * i + 4, 0, i + 2)
                step(2 * i + 5, 1, i + 2)
            for b in range(B - 2, B + 3):
                step(b, b % 2, b // 2)

            def turn_slots(t):
                pe.wait_ge(xs_in, (t + 1) * 16)
                turn(XT, xs).then_inc(tx_done, 1)

            def expert(e, i):
                first = pe.value_load(plan[0:1, bass.ds(e, 1)], min_val=0, max_val=MAXT)
                end = pe.value_load(plan[0:1, bass.ds(e + E, 1)], min_val=1, max_val=MAXT)
                after = value(pe, e + 1)
                pe.wait_ge(plan_done, 1)
                pe.wait_ge(w_in_low, after)
                pe.wait_ge(w_out_low, after)
                with pe.Fori(first, end) as t:
                    pe.wait_ge(xs_t_done, t + 1)
                    for m in range(FC):
                        for c in range(DC):
                            for w_part, x_part in PARTS:
                                ins = pe.matmul(HB[m // 2][:, (m % 2) * SLOT:(m % 2 + 1) * SLOT],
                                                w_in_sb[i][:, w_part, c, m * P:(m + 1) * P], xs_t[:, x_part, c, :],
                                                start=(c == 0 and (w_part, x_part) == PARTS[0]),
                                                stop=(c == DC - 1 and (w_part, x_part) == PARTS[-1]))
                        if m % 2:
                            ins.then_inc(h_done, 1)
                    turn_slots(t + 1)
                    pe.wait_ge(yb_read, t + 1)
                    for h_part, w_parts in ((0, (0, 1)), (1, (0,))):
                        for m in range(FC):
                            if m % 2 == 0 and h_part == 0:
                                pe.wait_ge(gelu_high, t * HP + (m // 2 + 1))
                            elif m % 2 == 0:
                                pe.wait_ge(hid_low, t * HP + (m // 2 + 1))
                            for s in range(SS):
                                for w_part in w_parts:
                                    ins = pe.matmul(YB[s][:, 0:D], hid_parts[:, h_part, m, s * P:(s + 1) * P],
                                                    w_out_sb[i][:, w_part, m, :],
                                                    start=(m == 0 and h_part == 0 and w_part == 0),
                                                    stop=(m == FC - 1 and h_part == 1))
                    ins.then_inc(y_done, 1)

            pe.wait_ge(rank_read, B)
            turn_slots(0)
            pe.wait_ge(plan_done, 1)
            with pe.Fori(0, NPAIR) as i:
                expert(2 * i, 0)
                expert(2 * i + 1, 1)


_OUT = (8, 256, 256)


def kernel(**inputs):
    import numpy as np
    import concourse.bacc as bacc
    from concourse.bass_utils import run_bass_kernel_spmd

    a = {k: np.asarray(v) for k, v in inputs.items()}
    ctx = a["ctx_1024"]
    b, nk, d = ctx.shape
    h, dh, p = 16, d // 16, 128
    gh = p // (2 * dh)
    by_head = ctx.transpose(0, 2, 1).reshape(b, h // gh, gh, dh, nk)
    keys = np.zeros((b, 2, gh, dh, h // gh, gh, nk), ctx.dtype)
    for i in range(gh):
        keys[:, :, i, :, :, i, :] = by_head[:, :, i].transpose(0, 2, 1, 3)[:, None]
    vals = np.ones((b, nk, h, 2 * dh), ctx.dtype)
    vals[..., :dh] = ctx.reshape(b, nk, h, dh)
    b_in = a["L0_ffn_b_in"]
    laid_out = {
        "x": a["x"],
        "keys_dram": keys.reshape(b, p, h, nk),
        "vals_dram": vals,
        "mask_cols": np.ascontiguousarray(a["mask_Bx1xS2_bk0"][:, 0, :].T),
        "scalars": np.concatenate([a[n].reshape(1) for n in ("L0_xattn_scale", "L0_xattn_log_C", "g_xattn", "g_ffn")]),
        "wo_t": np.ascontiguousarray(a["L0_xattn_W_out"].T),
        "w_gate": a["L0_ffn_W_gate"],
        "w_in": a["L0_ffn_W_in"],
        "b_in": np.ascontiguousarray(b_in.reshape(b_in.shape[0], -1, p).transpose(2, 0, 1)),
        "w_out": a["L0_ffn_W_out"],
        "b_out": a["L0_ffn_b_out"],
    }
    nc = bacc.Bacc("TRN2", target_bir_lowering=False, num_devices=1)
    aps = {n: nc.dram_tensor(n, v.shape, mybir.dt.from_np(v.dtype), kind="ExternalInput").ap()
           for n, v in laid_out.items()}
    out = nc.dram_tensor("out", _OUT, mybir.dt.float32, kind="ExternalOutput").ap()
    flamingo_layer(nc, out=out, **aps)
    r = run_bass_kernel_spmd(nc, [laid_out], core_ids=[0])
    return r.results[0]["out"]
```
